# Optimizing a Trainium2 kernel written in Bass

```python
import numpy as np
import jax
import jax.numpy as jnp

def _softmax(x, axis=-1):
    return jax.nn.softmax(x, axis=axis)

def _gelu(x):
    return jax.nn.gelu(x, approximate=True)

def _silu(x):
    return jax.nn.silu(x)

def _sigmoid(x):
    return jax.nn.sigmoid(x)

def _layernorm(x, axis=-1, eps=1e-05):
    m = jnp.mean(x, axis=axis, keepdims=True)
    v = jnp.var(x, axis=axis, keepdims=True)
    return (x - m) / jnp.sqrt(v + eps)

def _scatter_add(tgt, idx, src, axis=0):
    return tgt.at[idx].add(src)

def _segment_sum(src, seg, n):
    return jax.ops.segment_sum(src, seg, n)
kernel_name = 'mk_macaron_d1_jaxref_r8_faab82'

def setup_inputs(seed: int=0):
    np.random.seed(seed)
    _w = jnp.asarray

    def _L0_attn_setup():
        import jax, jax.numpy as jnp
        import numpy as np
        B, S, D = (2, 256, 256)
        H, HD = (16, 128)
        NEG_INF = -1e+30

        def _rope_tables(seq_len, head_dim):
            freqs = 1.0 / 10000.0 ** (np.arange(0, head_dim, 2, dtype=np.float32) / head_dim)
            pos = np.arange(seq_len, dtype=np.float32)
            ang = np.outer(pos, freqs)
            return (jnp.asarray(np.cos(ang)), jnp.asarray(np.sin(ang)))

        def _apply_rope(x, cos, sin):
            x1 = x[..., 0::2]
            x2 = x[..., 1::2]
            rx1 = x1 * cos - x2 * sin
            rx2 = x1 * sin + x2 * cos
            return jnp.stack([rx1, rx2], axis=-1).reshape(x.shape)
        key = jax.random.key(seed)
        ks = jax.random.split(key, 5)
        scale = 1.0 / np.sqrt(D)
        return {'x': jax.random.normal(ks[0], (B, S, D), dtype=jnp.float32), 'Wq': jax.random.normal(ks[1], (D, H * HD), dtype=jnp.float32) * scale, 'Wk': jax.random.normal(ks[2], (D, H * HD), dtype=jnp.float32) * scale, 'Wv': jax.random.normal(ks[3], (D, H * HD), dtype=jnp.float32) * scale, 'Wo': jax.random.normal(ks[4], (H * HD, D), dtype=jnp.float32) * scale}
    _L0_attn_in = _L0_attn_setup()

    def _L0_ffn_setup():
        import jax, jax.numpy as jnp
        import numpy as np
        NUM_EXPERTS = 4
        key = jax.random.key(seed)
        k1, k2, k3 = jax.random.split(key, 3)
        B, N, H = (8, 256, 256)
        E = NUM_EXPERTS
        I = H * 4 // E
        x = jax.random.normal(k1, (B, N, H), dtype=jnp.float32)
        gate_up_proj = jax.random.normal(k2, (E, H, 2 * I), dtype=jnp.float32) * 0.02
        down_proj = jax.random.normal(k3, (E, I, H), dtype=jnp.float32) * 0.02
        return {'x': x, 'gate_up_proj': gate_up_proj, 'down_proj': down_proj}
    _L0_ffn_in = _L0_ffn_setup()
    _d = {'L0_attn_x': _L0_attn_in['x'], 'L0_attn_Wq': _L0_attn_in['Wq'], 'L0_attn_Wk': _L0_attn_in['Wk'], 'L0_attn_Wv': _L0_attn_in['Wv'], 'L0_attn_Wo': _L0_attn_in['Wo'], 'L0_ffn_gate_up_proj': _L0_ffn_in['gate_up_proj'], 'L0_ffn_down_proj': _L0_ffn_in['down_proj']}
    _x0 = _d['L0_attn_x']
    _d['L0_attn_x'] = jax.random.normal(jax.random.fold_in(jax.random.key(seed), 1), (4, 1024, 256), dtype=_x0.dtype)
    del _x0
    return _d

def reference(L0_attn_x, L0_attn_Wq, L0_attn_Wk, L0_attn_Wv, L0_attn_Wo, L0_ffn_gate_up_proj, L0_ffn_down_proj):

    def _L0_attn_ref(x, Wq, Wk, Wv, Wo):
        import jax, jax.numpy as jnp
        import numpy as np
        B, S, D = (2, 256, 256)
        H, HD = (16, 128)
        NEG_INF = -1e+30

        def _rope_tables(seq_len, head_dim):
            freqs = 1.0 / 10000.0 ** (np.arange(0, head_dim, 2, dtype=np.float32) / head_dim)
            pos = np.arange(seq_len, dtype=np.float32)
            ang = np.outer(pos, freqs)
            return (jnp.asarray(np.cos(ang)), jnp.asarray(np.sin(ang)))

        def _apply_rope(x, cos, sin):
            x1 = x[..., 0::2]
            x2 = x[..., 1::2]
            rx1 = x1 * cos - x2 * sin
            rx2 = x1 * sin + x2 * cos
            return jnp.stack([rx1, rx2], axis=-1).reshape(x.shape)
        b, s, _ = x.shape
        cos, sin = _rope_tables(s, HD)

        def split_heads(t):
            return t.reshape(b, s, H, HD).transpose(0, 2, 1, 3)
        q = split_heads(x @ Wq)
        k = split_heads(x @ Wk)
        v = split_heads(x @ Wv)
        q = _apply_rope(q, cos, sin)
        k = _apply_rope(k, cos, sin)
        scale = 1.0 / np.sqrt(HD)
        scores = jnp.einsum('bhqd,bhkd->bhqk', q, k) * scale
        causal = jnp.triu(jnp.ones((s, s), dtype=bool), k=1)
        scores = jnp.where(causal[None, None], NEG_INF, scores)
        attn = jax.nn.softmax(scores, axis=-1)
        ctx = jnp.einsum('bhqk,bhkd->bhqd', attn, v)
        ctx = ctx.transpose(0, 2, 1, 3).reshape(b, s, H * HD)
        return ctx @ Wo

    def _L0_ffn_ref(x, gate_up_proj, down_proj):
        import jax, jax.numpy as jnp
        import numpy as np
        NUM_EXPERTS = 4
        B, N, H = x.shape
        E, _, two_I = gate_up_proj.shape
        I = two_I // 2
        G = N // E
        x4 = x.reshape(B, G, E, H)
        gu = jnp.einsum('bgeh,ehd->bged', x4, gate_up_proj)
        gate, up = (gu[..., :I], gu[..., I:])
        inter = jax.nn.silu(gate) * up
        out = jnp.einsum('bgei,eih->bgeh', inter, down_proj)
        return out.reshape(B, N, H)
    x = L0_attn_x
    x = x + 0.5 * _L0_ffn_ref(_layernorm(x, axis=-1), L0_ffn_gate_up_proj, L0_ffn_down_proj)
    x = x + _L0_attn_ref(_layernorm(x, axis=-1), L0_attn_Wq, L0_attn_Wk, L0_attn_Wv, L0_attn_Wo)
    x = x + 0.5 * _L0_ffn_ref(_layernorm(x, axis=-1), L0_ffn_gate_up_proj, L0_ffn_down_proj)
    return x

_drawn_inputs = setup_inputs


def setup_inputs(seed=0):
    import zlib

    import numpy as np

    out = dict(_drawn_inputs(seed))
    spreads = {}
    factors = {'L0_ffn_gate_up_proj': 3.498, 'L0_ffn_down_proj': 3.497}
    for name, (base, spread) in spreads.items():
        noise = np.random.default_rng([zlib.crc32(name.encode()), seed]).standard_normal(out[name].shape)
        drawn = base * np.exp(spread * noise) if base else spread * noise
        out[name] = jnp.asarray(drawn.astype(out[name].dtype))
    for name, factor in factors.items():
        out[name] = (out[name] * factor).astype(out[name].dtype)
    return out
```

```python
from contextlib import ExitStack

import concourse.bass as bass
import numpy as np
from concourse import mybir

ALU = mybir.AluOpType
ACT = mybir.ActivationFunctionType
AX = mybir.AxisListType
F32 = mybir.dt.float32
F32R = mybir.dt.float32r

P = 128
B, S, D = 4, 1024, 256
H, HD = 16, 128
E, I = 4, 256
EPS = 1e-5
NEG = -1e30
KT = D // P
CH = 512
NCH = S // CH
NT = S // P
PAIRS = H // 2
NPAIR = B * PAIRS
HALF = HD // 2


CTX_LO_DONE_CREDIT = 1
EXP_DONE_CREDIT = 3
INNER_DONE_CREDIT = 2
INNER_LO_CREDIT = 2
OUT_ADDED_CREDIT = 1
OUT_FILLED_CREDIT = 1
P_TURNED_CREDIT = 3
PT_LO_DONE_CREDIT = 2
STORED_CREDIT = 16
XNT_STORED_CREDIT = 32
Y_ADDED_CREDIT = 2
Y_DONE_CREDIT = 2


def passes(hi_a, lo_a, hi_b, lo_b):
    return (hi_a, hi_b), (hi_a, lo_b), (lo_a, hi_b)


def f(ap):
    return ap.bitcast(F32)


def ffn_stage(nc, tag, src, dst, gate_up, down, ident, xnt):
    post = xnt is not None
    with ExitStack() as ctx:
        def sb(name, shape, dt=F32):
            return ctx.enter_context(nc.sbuf_tensor(tag + name, shape, dt))

        def ps(name, shape):
            return ctx.enter_context(nc.psum_tensor(tag + name, shape, F32))

        def signal(name):
            return ctx.enter_context(nc.semaphore(tag + name))

        gu_raw = sb("gu_raw", [P, E, KT, 2 * I])
        gu_hi = sb("gu_hi", [P, E, KT, 2 * I], F32R)
        gu_lo = sb("gu_lo", [P, E, KT, 2 * I], F32R)
        dn_raw = sb("dn_raw", [P, E, KT, D])
        dn_hi = sb("dn_hi", [P, E, KT, D], F32R)
        dn_lo = sb("dn_lo", [P, E, KT, D], F32R)
        idn = sb("idn", [P, P])
        x_in = sb("x_in", [P, NCH, E, D])
        x_res = sb("x_res", [P, NCH, E, D])
        x_out = sb("x_out", [P, NCH, E, D])
        xn = sb("xn", [P, NCH, E, D])
        xn_out = sb("xn_out", [P, NCH, E, D])
        xt_hi = sb("xt_hi", [P, KT, E, NCH, P], F32R)
        xt_lo = sb("xt_lo", [P, KT, E, NCH, P], F32R)
        xo_hi = sb("xo_hi", [P, KT, S], F32R)
        xo_lo = sb("xo_lo", [P, KT, S], F32R)
        stats = sb("stats", [P, 2, 8, 6])
        mv = sb("mv", [P, 2, 8, 2])
        var = sb("var", [P, 2, 8])
        rstd = sb("rstd", [P, 2, 8])
        mhalf = sb("mhalf", [P, 8])
        sig = sb("sig", [P, 2, CH])
        silu_g = sb("silu_g", [P, 2, CH])
        inner = sb("inner", [P, 2, CH])
        in_hi = sb("in_hi", [P, 2, 2, D], F32R)
        in_lo = sb("in_lo", [P, 2, 2, D], F32R)
        ps_t = ps("ps_t", [P, 2, CH])
        ps_g = ps("ps_g", [P, 2, CH])
        ps_u = ps("ps_u", [P, 2, CH])
        ps_y = ps("ps_y", [P, 2, CH])

        w_in = [signal(f"w_in{e}") for e in range(E)]
        id_in = signal("id_in")
        w_hi = signal("w_hi")
        w_lo = signal("w_lo")
        x_loaded = signal("x_loaded")
        half_set = signal("half_set")
        stats_done = signal("stats_done")
        var_done = signal("var_done")
        rstd_done = signal("rstd_done")
        xn_done = signal("xn_done")
        turned = signal("turned")
        turned_hi = signal("turned_hi")
        turned_lo = signal("turned_lo")
        gu_done = signal("gu_done")
        sigmoid_done = signal("sigmoid_done")
        silu_step = signal("silu_step")
        inner_done = signal("inner_done")
        inner_hi = signal("inner_hi")
        inner_lo = signal("inner_lo")
        y_done = signal("y_done")
        y_added = signal("y_added")
        res_copied = signal("res_copied")
        stored = signal("stored")
        xnt_stored = signal("xnt_stored")
        sp_own = signal("sp_own")
        dve_own = signal("dve_own")

        groups = 8 if post else 4
        norms = 2 if post else 1

        def xt_part(t, g):
            return t[:, g // 2, 2 * (g % 2):2 * (g % 2) + 2].rearrange("p e c q -> p (e c q)")

        def xo_part(t, g):
            return t[:, g // 2, CH * (g % 2):CH * (g % 2) + CH].rearrange("p (q e) -> p e q", e=E)

        block = ctx.enter_context(nc.Block())

        @block.sync
        def _(sp):
            sp.sem_inc(stored, STORED_CREDIT)
            if post:
                sp.sem_inc(xnt_stored, XNT_STORED_CREDIT)
            sp.dma_start(x_in[:, :, :, :], src[0].rearrange("(c p e) d -> p c e d", c=NCH, e=E)).then_inc(x_loaded, 16)
            sp.dma_start(idn[:, :], ident).then_inc(id_in, 16)
            for e in range(E):
                sp.dma_start(gu_raw[:, e], gate_up[e].rearrange("(k p) n -> p k n", p=P)).then_inc(w_in[e], 16)
                sp.dma_start(dn_raw[:, e], down[e].rearrange("(k p) n -> p k n", p=P)).then_inc(w_in[e], 16)

            def batch(k, last):
                if not last:
                    sp.wait_ge(res_copied, k + 1)
                    sp.sem_inc(sp_own, 1)
                    sp.dma_start(x_in[:, :, :, :], src[k + 1].rearrange("(c p e) d -> p c e d", c=NCH, e=E)).then_inc(x_loaded, 16)
                sp.wait_ge(y_added, E * k + E + Y_ADDED_CREDIT)
                sp.sem_inc(sp_own, 1)
                sp.dma_start(dst[k].rearrange("(c p e) d -> p c e d", c=NCH, e=E), x_out[:, :, :, :]).then_inc(stored, 16)
                if post:
                    sp.wait_ge(turned_lo, groups * k + (8 if last else 12))
                    sp.sem_inc(sp_own, 1)
                    sp.dma_start(xnt[k, 0], f(xo_hi[:, :, :])).then_inc(xnt_stored, 16)
                    sp.dma_start(xnt[k, 1], f(xo_lo[:, :, :])).then_inc(xnt_stored, 16)

            with sp.Fori(0, B - 1) as k:
                batch(k, False)
            batch(B - 1, True)
            sp.wait_ge(stored, 16 * B + STORED_CREDIT)
            if post:
                sp.wait_ge(xnt_stored, 32 * B + XNT_STORED_CREDIT)

        @block.gpsimd
        def _(pool):
            pool.sem_inc(inner_lo, INNER_LO_CREDIT)
            pool.memset(mhalf[:, :], -0.5).then_inc(half_set, 1)
            pool.wait_ge(half_set, 1)

            def root(n, slot):
                pool.wait_ge(var_done, n + 1)
                pool.tensor_tensor(rstd[:, slot], var[:, slot], mhalf[:, :], ALU.pow).then_inc(rstd_done, 1)

            def batch(k, last):
                for e in range(E):
                    pool.wait_ge(inner_hi, E * k + e + 1)
                    pool.wait_ge(y_done, E * k + e - 1 + Y_DONE_CREDIT)
                    pool.tensor_tensor(in_lo[:, e % 2].rearrange("p a b -> p (a b)"), inner[:, e % 2],
                                       f(in_hi[:, e % 2].rearrange("p a b -> p (a b)")), ALU.subtract).then_inc(inner_lo, 1)
                    if e == 0 and not last:
                        root(norms * k + 1, 0)
                if post:
                    root(norms * k + (1 if last else 2), 1)

            root(0, 0)
            with pool.Fori(0, B - 1) as k:
                batch(k, False)
            batch(B - 1, True)

        @block.scalar
        def _(act):
            for e in range(E):
                act.wait_ge(w_in[e], 32)
                act.activation(gu_hi[:, e], gu_raw[:, e], ACT.Copy).then_inc(w_hi, 1)
                act.activation(dn_hi[:, e], dn_raw[:, e], ACT.Copy).then_inc(w_hi, 1)

            def turn_hi(g0, out):
                for g in range(4):
                    act.wait_ge(turned, g0 + g + 1)
                    act.activation(out(g), ps_t[:, g % 2], ACT.Copy).then_inc(turned_hi, 1)

            def batch(k, last):
                def sigmoid(e):
                    act.wait_ge(gu_done, E * k + e + 1)
                    act.wait_ge(inner_done, E * k + e - 1 + INNER_DONE_CREDIT)
                    act.activation(sig[:, e % 2], ps_g[:, e % 2], ACT.Sigmoid).then_inc(sigmoid_done, 1)

                def half(e):
                    act.wait_ge(y_done, E * k + e - 1 + Y_DONE_CREDIT)
                    act.wait_ge(inner_done, E * k + e + 1 + INNER_DONE_CREDIT)
                    act.activation(in_hi[:, e % 2].rearrange("p a b -> p (a b)"), inner[:, e % 2],
                                   ACT.Copy).then_inc(inner_hi, 1)

                sigmoid(0)
                for e in range(1, E):
                    sigmoid(e)
                    half(e - 1)
                half(E - 1)
                if not last:
                    turn_hi(groups * k + 4, lambda g: xt_part(xt_hi, g))
                if post:
                    act.wait_ge(xnt_stored, 32 * k + XNT_STORED_CREDIT)
                    turn_hi(groups * k + (4 if last else 8), lambda g: xo_part(xo_hi, g))

            turn_hi(0, lambda g: xt_part(xt_hi, g))
            with act.Fori(0, B - 1) as k:
                batch(k, False)
            batch(B - 1, True)

        @block.vector
        def _(dve):
            dve.sem_inc(inner_done, INNER_DONE_CREDIT)
            dve.sem_inc(y_added, Y_ADDED_CREDIT)

            def norm_stats(x, n, slot):
                for t in range(8):
                    last = dve.bn_stats(stats[:, slot, t], x[:, t // E, t % E])
                last.then_inc(stats_done, 1)
                dve.wait_ge(stats_done, 2 * n + 1)
                dve.sem_inc(dve_own, 1)
                for t in range(8):
                    last = dve.bn_aggr(mv[:, slot, t], stats[:, slot, t])
                last.then_inc(stats_done, 1)
                dve.wait_ge(stats_done, 2 * n + 2)
                dve.tensor_scalar(var[:, slot], mv[:, slot, :, 1], EPS, None, ALU.add).then_inc(var_done, 1)

            def norm_apply(x, out, n, slot):
                dve.wait_ge(rstd_done, n + 1)
                for t in range(8):
                    dve.tensor_scalar(out[:, t // E, t % E], x[:, t // E, t % E], mv[:, slot, t, 0:1],
                                      rstd[:, slot, t:t + 1], ALU.subtract, ALU.mult).then_inc(xn_done, 1)

            def turn_lo(g0, hi, lo):
                for g in range(4):
                    dve.wait_ge(turned_hi, g0 + g + 1)
                    dve.tensor_tensor(lo(g), ps_t[:, g % 2].rearrange("p (e q) -> p e q", q=P) if len(lo(g).shape) == 3 else ps_t[:, g % 2],
                                      f(hi(g)), ALU.subtract).then_inc(turned_lo, 1)

            def silu(k, e):
                n = E * k + e
                dve.wait_ge(sigmoid_done, n + 1)
                dve.tensor_tensor(silu_g[:, e % 2], ps_g[:, e % 2], sig[:, e % 2], ALU.mult).then_inc(silu_step, 1)
                dve.wait_ge(silu_step, n + 1)
                dve.wait_ge(inner_lo, n - 1 + INNER_LO_CREDIT)
                dve.tensor_tensor(inner[:, e % 2], ps_u[:, e % 2], silu_g[:, e % 2], ALU.mult).then_inc(inner_done, 1)

            def add_y(k, e):
                if e == 0:
                    dve.wait_ge(stored, 16 * k + STORED_CREDIT)
                dve.wait_ge(y_done, E * k + e + 1 + Y_DONE_CREDIT)
                dve.scalar_tensor_tensor(out=x_out[:, :, e], in0=ps_y[:, e % 2].rearrange("p (c d) -> p c d", c=NCH),
                                         scalar=0.5, in1=x_res[:, :, e], op0=ALU.mult, op1=ALU.add).then_inc(y_added, 1)

            def split_weights(e):
                dve.wait_ge(w_hi, 2 * e + 1)
                dve.tensor_tensor(gu_lo[:, e], gu_raw[:, e], f(gu_hi[:, e]), ALU.subtract).then_inc(w_lo, 1)
                dve.wait_ge(w_hi, 2 * e + 2)
                dve.tensor_tensor(dn_lo[:, e], dn_raw[:, e], f(dn_hi[:, e]), ALU.subtract).then_inc(w_lo, 1)

            def keep_residual(k):
                dve.tensor_copy(x_res[:, :, :, :], x_in[:, :, :, :]).then_inc(res_copied, 1)

            def batch(k, last):
                silu(k, 0)
                if not last:
                    dve.wait_ge(x_loaded, 16 * k + 32)
                    norm_stats(x_in, norms * k + 1, 0)
                silu(k, 1)
                add_y(k, 0)
                if not last:
                    norm_apply(x_in, xn, norms * k + 1, 0)
                silu(k, 2)
                add_y(k, 1)
                silu(k, 3)
                add_y(k, 2)
                if not last:
                    turn_lo(groups * k + 4, lambda g: xt_part(xt_hi, g), lambda g: xt_part(xt_lo, g))
                add_y(k, 3)
                if not last:
                    dve.wait_ge(y_added, E * k + E + Y_ADDED_CREDIT)
                    keep_residual(k + 1)
                if post:
                    n = norms * k + (1 if last else 2)
                    dve.wait_ge(y_added, E * k + E + Y_ADDED_CREDIT)
                    norm_stats(x_out, n, 1)
                    norm_apply(x_out, xn_out, n, 1)
                    dve.wait_ge(xnt_stored, 32 * k + XNT_STORED_CREDIT)
                    turn_lo(groups * k + (4 if last else 8), lambda g: xo_part(xo_hi, g), lambda g: xo_part(xo_lo, g))

            dve.wait_ge(x_loaded, 16)
            norm_stats(x_in, 0, 0)
            norm_apply(x_in, xn, 0, 0)
            keep_residual(0)
            split_weights(0)
            turn_lo(0, lambda g: xt_part(xt_hi, g), lambda g: xt_part(xt_lo, g))
            for e in range(1, E):
                split_weights(e)
            with dve.Fori(0, B - 1) as k:
                batch(k, False)
            batch(B - 1, True)

        @block.tensor
        def _(pe):
            pe.sem_inc(y_done, Y_DONE_CREDIT)

            def turn_in(n, g0):
                pe.wait_ge(xn_done, 8 * n + 8)
                for g in range(4):
                    if not (isinstance(g0, int) and g0 + g < 2):
                        pe.wait_ge(turned_lo, g0 + g - 1)
                    for j in range(4):
                        e, c = 2 * (g % 2) + j // 2, j % 2
                        last = pe.transpose(ps_t[:, g % 2, P * j:P * j + P], xn[:, c, e, P * (g // 2):P * (g // 2) + P], idn[:, :])
                    last.then_inc(turned, 1)

            def turn_out(n, g0):
                pe.wait_ge(xn_done, 8 * n + 8)
                for g in range(4):
                    pe.wait_ge(turned_lo, g0 + g - 1)
                    for e in range(E):
                        last = pe.transpose(ps_t[:, g % 2, P * e:P * e + P],
                                            xn_out[:, g % 2, e, P * (g // 2):P * (g // 2) + P], idn[:, :])
                    last.then_inc(turned, 1)

            def gate_up_of(k, e):
                pe.wait_ge(inner_done, E * k + e - 1 + INNER_DONE_CREDIT)
                for out, col in ((ps_g, 0), (ps_u, I)):
                    for m in range(2):
                        n = 0
                        for kt in range(KT):
                            cols = slice(col + P * m, col + P * m + P)
                            x_h = xt_hi[:, kt, e].rearrange("p c q -> p (c q)")
                            x_l = xt_lo[:, kt, e].rearrange("p c q -> p (c q)")
                            for w, x in passes(gu_hi[:, e, kt, cols], gu_lo[:, e, kt, cols], x_h, x_l):
                                last = pe.matmul(out[:, e % 2, D * m:D * m + D], w, x, start=n == 0, stop=n == 3 * KT - 1)
                                n += 1
                last.then_inc(gu_done, 1)

            def down_of(k, e):
                pe.wait_ge(inner_lo, E * k + e + 1 + INNER_LO_CREDIT)
                pe.wait_ge(y_added, E * k + e - 1 + Y_ADDED_CREDIT)
                for c in range(NCH):
                    n = 0
                    for m in range(2):
                        i_h, i_l = in_hi[:, e % 2, m, P * c:P * c + P], in_lo[:, e % 2, m, P * c:P * c + P]
                        for i, w in passes(i_h, i_l, dn_hi[:, e, m], dn_lo[:, e, m]):
                            last = pe.matmul(ps_y[:, e % 2, D * c:D * c + D], i, w, start=n == 0, stop=n == 5)
                            n += 1
                last.then_inc(y_done, 1)

            def batch(k, last):
                pe.wait_ge(turned_lo, groups * k + 4)
                gate_up_of(k, 0)
                gate_up_of(k, 1)
                down_of(k, 0)
                gate_up_of(k, 2)
                down_of(k, 1)
                gate_up_of(k, 3)
                down_of(k, 2)
                if not last:
                    turn_in(norms * k + 1, groups * k + 4)
                down_of(k, 3)
                if post:
                    turn_out(norms * k + (1 if last else 2), groups * k + (4 if last else 8))

            pe.wait_ge(id_in, 16)
            turn_in(0, 0)
            pe.wait_ge(w_lo, 2 * E)
            with pe.Fori(0, B - 1) as k:
                batch(k, False)
            batch(B - 1, True)




STEPS = 2 * NT


def chunks(s):
    h, i = divmod(s, NT)
    first = 12 * h + (i if i < 4 else 4 + 2 * (i - 4))
    return [(first + c, c, min(CH, P * (i + 1) - CH * c)) for c in range(i // 4 + 1)]


NCHUNK = sum(len(chunks(s)) for s in range(STEPS))
QK_ORDER = [("q", 0), ("q", 1), ("k", 0), ("k", 1), ("q", 2), ("q", 3), ("k", 2), ("k", 3)]
QKV_ORDER = QK_ORDER + [("v", 0), ("v", 1), ("v", 2), ("v", 3)]
QKV_FILLS = dict(zip((0, 2, 3, 4, 6, 7, 8, 10, 11, 12, 14, 15), QKV_ORDER))
OUT_FILLS = {1: 0, 2: 1, 5: 2, 6: 3, 9: 4, 10: 5, 13: 6, 14: 7}
FILLS = []
for _s in range(STEPS):
    if _s in QKV_FILLS:
        FILLS.append(QKV_FILLS[_s])
    if _s in OUT_FILLS:
        FILLS.append(("o", OUT_FILLS[_s]))
WEIGHTS = [(1, "v"), (7, "o"), (9, "q"), (12, "k")]
W_INDEX = {w: n for n, (_, w) in enumerate(WEIGHTS)}
W_FIRST = ["q", "k", "v", "q", "k"]
W_BEFORE = len(W_FIRST)
QK_SPLITS = [(0, 0, 1, 0, 0), (1, 0, 1, 1, 0), (3, 0, 1, 0, 1), (6, 0, 1, 1, 1),
             (8, 1, 0, 0, 0), (10, 1, 0, 1, 0), (13, 1, 0, 0, 1), (14, 1, 0, 1, 1)]
QK_BEFORE = 4
RDEN_BEFORE = 1


def bank(kind, idx, m):
    if isinstance(m, int) and m == 0:
        return idx % 2
    return FILLS.index((kind, idx)) % 2


def attention_stage(nc, src, dst, xnt, wq, wk, wv, wo, rope, mask, ident):
    with ExitStack() as ctx:
        def sb(name, shape, dt=F32):
            return ctx.enter_context(nc.sbuf_tensor(name, shape, dt))

        def ps(name, shape):
            return ctx.enter_context(nc.psum_tensor(name, shape, F32))

        def signal(name):
            return ctx.enter_context(nc.semaphore(name))

        raw = {w: sb(f"raw_{w}", [P, KT, 2 * HD]) for w in "qkvo"}
        w_hi = {w: sb(f"w_hi_{w}", [P, KT, 2 * HD], F32R) for w in "qkvo"}
        w_lo = {w: sb(f"w_lo_{w}", [P, KT, 2 * HD], F32R) for w in "qkvo"}
        xt_hi = sb("xt_hi", [P, KT, S], F32R)
        xt_lo = sb("xt_lo", [P, KT, S], F32R)
        x = sb("x", [P, NT, D])
        cs = sb("cs", [P, 4, 2, 256])
        msk = sb("msk", [P, P])
        idn = sb("idn", [P, P])
        prod_a = sb("prod_a", [P, 2, 2, 256])
        prod_b = sb("prod_b", [P, 2, 2, 256])
        rot2 = sb("rot2", [P, 2, CH])
        qk_raw = sb("qk_raw", [P, 2, 2, S])
        qk_hi = sb("qk_hi", [P, 2, 2, S], F32R)
        qk_lo = sb("qk_lo", [P, 2, 2, S], F32R)
        v_raw = sb("v_raw", [P, NT, 2 * HD])
        v_hi = sb("v_hi", [P, NT, 2 * HD], F32R)
        v_lo = sb("v_lo", [P, NT, 2 * HD], F32R)
        probs = sb("probs", [P, 2, S])
        pt_hi = [sb(f"pt_hi{c}", [P, 4 * (c + 1), CH], F32R) for c in range(2)]
        pt_lo = [sb(f"pt_lo{c}", [P, 4 * (c + 1), CH], F32R) for c in range(2)]
        ctx_hi = sb("ctx_hi", [P, CH], F32R)
        ctx_lo = sb("ctx_lo", [P, CH], F32R)
        part_max = sb("part_max", [P, 2, 4])
        neg_max = sb("neg_max", [P, 4])
        den = sb("den", [P, 2, NT, 2])
        den_sum = sb("den_sum", [P, 2, NT])
        rden = sb("rden", [P, 2, NT])
        ps_s = ps("ps_s", [P, 3, CH])
        ps_t = ps("ps_t", [P, 2, CH])
        ps_c = ps("ps_c", [P, CH])
        ps_f = ps("ps_f", [P, 2, CH])

        const_in = signal("const_in")
        raw_in = {w: signal(f"raw_in_{w}") for w in "qkvo"}
        q_scaled = signal("q_scaled")
        w_hi_done = signal("w_hi_done")
        w_lo_done = signal("w_lo_done")
        xt_in = [signal(f"xt_in{half}") for half in range(2)]
        x_in = [signal(f"x_in{c}") for c in range(2)]
        x_out = [signal(f"x_out{c}") for c in range(2)]
        zeroed = signal("zeroed")
        qk_filled = signal("qk_filled")
        v_filled = signal("v_filled")
        out_filled = signal("out_filled")
        prod_done = signal("prod_done")
        rot_done = signal("rot_done")
        parted = signal("parted")
        shifted = [signal(f"shifted{g}") for g in range(4)]
        qk_hi_done = signal("qk_hi_done")
        qk_lo_done = signal("qk_lo_done")
        v_raw_done = signal("v_raw_done")
        v_hi_done = signal("v_hi_done")
        v_lo_done = signal("v_lo_done")
        scored = signal("scored")
        part_done = signal("part_done")
        max_done = signal("max_done")
        exp_done = signal("exp_done")
        p_turned = signal("p_turned")
        pt_hi_done = signal("pt_hi_done")
        pt_lo_done = signal("pt_lo_done")
        pv_done = signal("pv_done")
        ctx_hi_done = signal("ctx_hi_done")
        ctx_lo_done = signal("ctx_lo_done")
        den_summed = signal("den_summed")
        rden_done = signal("rden_done")
        out_added = signal("out_added")
        sp_own = signal("sp_own")
        dve_own = signal("dve_own")

        def batches(eng, body):
            with eng.Fori(0, B) as b:
                body(b * PAIRS, b, "first")
                with eng.Fori(1, PAIRS - 1) as p:
                    body(b * PAIRS + p, b, "middle")
                body(b * PAIRS + PAIRS - 1, b, "last")

        def weight_view(t, w):
            return t[:, :, :].rearrange("p k (two f) -> p k two f", two=2) if w in "qk" else t[:, :, :]

        def raw_view(w):
            return raw[w][:, :, :].rearrange("p k (f two) -> p k two f", two=2) if w in "qk" else raw[w][:, :, :]

        block = ctx.enter_context(nc.Block())

        @block.sync
        def _(sp):
            w_dram = {"q": wq, "k": wk, "v": wv}

            def load_raw(w, pair):
                if w == "o":
                    view = wo[bass.ds(pair * 2 * HD, 2 * HD), :].rearrange("(h p) d -> p h d", p=P)
                else:
                    view = w_dram[w][:, bass.ds(pair * 2 * HD, 2 * HD)].rearrange("(k p) n -> p k n", p=P)
                sp.dma_start(raw[w][:, :, :], view).then_inc(raw_in[w], 16)

            def load_xt(batch):
                for half in range(2):
                    toks = slice(CH * half, CH * half + CH)
                    sp.dma_start(f(xt_hi[:, :, toks]), xnt[batch, 0][:, :, toks]).then_inc(xt_in[half], 16)
                    sp.dma_start(f(xt_lo[:, :, toks]), xnt[batch, 1][:, :, toks]).then_inc(xt_in[half], 16)

            def shift(m, g):
                sp.wait_ge(rot_done, 8 * m + 2 * g + 2)
                sp.sem_inc(sp_own, 1)
                kind, cols = g % 2, slice(CH * (g // 2), CH * (g // 2) + CH)
                sp.dma_start(qk_raw[HALF:P, kind, 1, cols], qk_raw[HALF:P, kind, 0, cols]).then_inc(parted, 16)
                sp.dma_start(qk_raw[0:HALF, kind, 1, cols], rot2[HALF:P, g % 2]).then_inc(shifted[g], 16)
                sp.wait_ge(parted, 16 * (4 * m + g + 1))
                sp.sem_inc(sp_own, 1)
                sp.dma_start(qk_raw[HALF:P, kind, 0, cols], rot2[0:HALF, g % 2]).then_inc(shifted[g], 16)

            def rows(t, b, c):
                return t[b].rearrange("(t p) d -> p t d", p=P)[:, 4 * c:4 * c + 4]

            def turn_over_x(n, b, c, store):
                sp.wait_ge(out_added, 8 * n + 2 * c + 2 + OUT_ADDED_CREDIT)
                sp.sem_inc(sp_own, 1)
                if store:
                    sp.dma_start(rows(dst, b - 1, c), x[:, 4 * c:4 * c + 4]).then_inc(x_out[c], 16)
                    sp.wait_ge(x_out[c], 16 * b)
                    sp.sem_inc(sp_own, 1)
                sp.dma_start(x[:, 4 * c:4 * c + 4], rows(src, b, c)).then_inc(x_in[c], 16)

            def body(n, b, p, kind, store=True):
                def next_raw(w, at):
                    sp.wait_ge(w_lo_done, W_BEFORE + 4 * n + W_INDEX[w] + 1)
                    sp.sem_inc(sp_own, 1)
                    load_raw(w, (p + at) % PAIRS)

                if kind == "last":
                    sp.wait_ge(v_filled, 4 * n + 4)
                    sp.sem_inc(sp_own, 1)
                    load_xt((b + 1) % B)
                next_raw("v", 2)
                if kind == "first":
                    turn_over_x(n, b, 0, store)
                shift(n + 1, 0)
                if kind == "first":
                    turn_over_x(n, b, 1, store)
                shift(n + 1, 1)
                next_raw("o", 1)
                shift(n + 1, 2)
                next_raw("q", 3)
                shift(n + 1, 3)
                next_raw("k", 3)

            def batch(b, store):
                body(b * PAIRS, b, 0, "first", store)
                with sp.Fori(1, PAIRS - 1) as p:
                    body(b * PAIRS + p, b, p, "middle")
                body(b * PAIRS + PAIRS - 1, b, PAIRS - 1, "last")

            load_xt(0)
            for w in "qkv":
                load_raw(w, 0)
            sp.dma_start(cs[:, :, :, :], rope).then_inc(const_in, 16)
            sp.dma_start(msk[:, :], mask).then_inc(const_in, 16)
            sp.dma_start(idn[:, :], ident).then_inc(const_in, 16)
            load_raw("o", 0)
            for n, w in enumerate(W_FIRST[:3]):
                sp.wait_ge(w_lo_done, n + 1)
                load_raw(w, 1)
            for g in range(4):
                shift(0, g)
            for n, w in enumerate(W_FIRST[3:]):
                sp.wait_ge(w_lo_done, 3 + n + 1)
                load_raw(w, 2)
            batch(0, False)
            with sp.Fori(1, B) as b:
                batch(b, True)
            for c in range(2):
                sp.wait_ge(out_added, 8 * NPAIR + 2 * c + 2 + OUT_ADDED_CREDIT)
                sp.dma_start(rows(dst, B - 1, c), x[:, 4 * c:4 * c + 4]).then_inc(x_out[c], 16)
            for c in range(2):
                sp.wait_ge(x_out[c], 16 * B)
            for w in "qkvo":
                sp.wait_ge(raw_in[w], 16 * (NPAIR + {"q": 3, "k": 3, "v": 2, "o": 1}[w]))

        @block.gpsimd
        def _(pool):
            def weight_lo(w, count, used, n_used):
                pool.wait_ge(w_hi_done, count)
                if used is not None:
                    pool.wait_ge(used, n_used)
                pool.tensor_tensor(weight_view(w_lo[w], w), raw_view(w), weight_view(f(w_hi[w][:, :, :]), w),
                                   ALU.subtract).then_inc(w_lo_done, 1)

            def rotate(m, idx):
                g = idx // 2
                kind, t = "qk".index(QK_ORDER[idx][0]), QK_ORDER[idx][1]
                cols = slice(256 * t, 256 * t + 256)
                pool.wait_ge(prod_done, 8 * m + idx + 1)
                if idx % 2 == 0 and not isinstance(m, int):
                    pool.wait_ge(qk_lo_done, QK_BEFORE + 8 * (m - 1) + g + 1)
                if idx % 2 == 0:
                    before = 32 * (m + 1) if g >= 2 else 32 * m
                    if not (isinstance(before, int) and before == 0):
                        pool.wait_ge(shifted[(g + 2) % 4], before)
                pool.tensor_tensor(qk_raw[:, kind, 0, cols], prod_a[:, idx % 2, 0], prod_a[:, idx % 2, 1], ALU.subtract)
                pool.tensor_tensor(rot2[:, g % 2, 256 * (t % 2):256 * (t % 2) + 256], prod_b[:, idx % 2, 0],
                                   prod_b[:, idx % 2, 1], ALU.add).then_inc(rot_done, 1)

            def qk_low(count, h, kind, half):
                toks = slice(CH * half, CH * half + CH)
                pool.wait_ge(qk_hi_done, count)
                pool.tensor_tensor(qk_lo[:, kind, h, toks], qk_raw[:, kind, h, toks], f(qk_hi[:, kind, h, toks]),
                                   ALU.subtract).then_inc(qk_lo_done, 1)

            def v_low(m, h):
                pool.wait_ge(v_hi_done, 2 * m + h + 1)
                cols = slice(HD * h, HD * h + HD)
                pool.tensor_tensor(v_lo[:, :, cols], v_raw[:, :, cols], f(v_hi[:, :, cols]),
                                   ALU.subtract).then_inc(v_lo_done, 1)

            def body(n, b, kind_of_body):
                for s in range(STEPS):
                    for j, (step, _, h, kind, half) in enumerate(QK_SPLITS):
                        if step == s:
                            qk_low(QK_BEFORE + 8 * n + j + 1, h, kind, half)
                    if s in QKV_FILLS and QKV_FILLS[s][0] != "v":
                        rotate(n + 1, QK_ORDER.index(QKV_FILLS[s]))
                    if s == 2:
                        v_low(n, 0)
                    if s == 5:
                        v_low(n, 1)
                    for idx, (step, w) in enumerate(WEIGHTS):
                        if step == s:
                            used, count = {"v": (v_filled, 4 * n + 4), "o": (out_filled, 8 * n + 4 + OUT_FILLED_CREDIT),
                                           "q": (qk_filled, 8 * n + 14), "k": (qk_filled, 8 * n + 16)}[w]
                            weight_lo(w, W_BEFORE + 4 * n + idx + 1, used, count)

            pool.memset(f(pt_hi[1][:, :, :]), 0.0).then_inc(zeroed, 1)
            pool.memset(f(v_lo[:, :, HD:]), 0.0).then_inc(zeroed, 1)
            for n, w in enumerate(W_FIRST):
                if n == 3:
                    for idx in range(8):
                        rotate(0, idx)
                    for j in range(4):
                        qk_low(j + 1, 0, j % 2, j // 2)
                weight_lo(w, n + 1, qk_filled if n >= 3 else None, 8)
            batches(pool, body)

        @block.scalar
        def _(act):
            def v_copy(m, idx):
                act.wait_ge(v_filled, 4 * m + idx + 1)
                act.activation(v_raw[:, 2 * idx:2 * idx + 2].rearrange("p t d -> p (t d)"), ps_f[:, bank("v", idx, m)],
                               ACT.Copy).then_inc(v_raw_done, 1)

            def qk_high(m, h, kind, half, n_scored):
                g = 2 * half + kind
                toks = slice(CH * half, CH * half + CH)
                act.wait_ge(rot_done, 8 * m + 2 * g + 2)
                act.wait_ge(shifted[g], 32 * (m + 1))
                if n_scored is not None:
                    act.wait_ge(scored, n_scored)
                act.activation(qk_hi[:, kind, h, toks], qk_raw[:, kind, h, toks], ACT.Copy).then_inc(qk_hi_done, 1)

            def v_high(m, h, sig, n):
                act.wait_ge(v_raw_done, 4 * m + 4)
                act.wait_ge(sig, n)
                cols = slice(HD * h, HD * h + HD)
                act.activation(v_hi[:, :, cols], v_raw[:, :, cols], ACT.Copy).then_inc(v_hi_done, 1)

            def exps(n, s, slot_used=True):
                act.wait_ge(max_done, STEPS * n + s + 1)
                if slot_used:
                    before = chunks(s - 2)[-1][0] if s >= 2 else chunks(s - 2 + STEPS)[-1][0] - NCHUNK
                    act.wait_ge(p_turned, NCHUNK * n + before + 1 + P_TURNED_CREDIT)
                h, i = divmod(s, NT)
                for ci, c, k in chunks(s):
                    act.activation(probs[:, s % 2, CH * c:CH * c + k], ps_s[:, ci % 3, 0:k], ACT.Exp,
                                   bias=neg_max[:, s % 4:s % 4 + 1],
                                   accum_out=den[:, h, i, c:c + 1]).then_inc(exp_done, 1)

            def pt_high(n, s, ci, c, k):
                i = s % NT
                act.wait_ge(p_turned, NCHUNK * n + ci + 1 + P_TURNED_CREDIT)
                act.activation(pt_hi[i // 4][:, 4 * c:4 * c + k // P, P * (i % 4):P * (i % 4) + P],
                               ps_t[:, ci % 2, 0:k].rearrange("p (j q) -> p j q", q=P), ACT.Copy).then_inc(pt_hi_done, 1)

            def ctx_high(n, k):
                act.wait_ge(pv_done, 4 * n + k + 1)
                act.wait_ge(out_filled, 8 * n + 2 * k + 2 + OUT_FILLED_CREDIT)
                act.activation(ctx_hi[:, :], ps_c[:, :], ACT.Copy).then_inc(ctx_hi_done, 1)

            def body(n, b, kind_of_body):
                for s in range(STEPS):
                    if s in QKV_FILLS and QKV_FILLS[s][0] == "v":
                        if QKV_FILLS[s][1] == 0:
                            act.wait_ge(v_lo_done, 2 * n + 2)
                        v_copy(n + 1, QKV_FILLS[s][1])
                    m, nxt = (n, s + 1) if s + 1 < STEPS else (n + 1, 0)
                    if len(chunks(nxt)) == 1:
                        exps(m, nxt)
                    for ci, c, k in chunks(s):
                        pt_high(n, s, ci, c, k)
                    if len(chunks(nxt)) > 1:
                        exps(m, nxt)
                    if s % 4 == 3:
                        ctx_high(n, s // 4)
                    for step, w in WEIGHTS:
                        if step == s:
                            if w == "q":
                                act.wait_ge(q_scaled, n + 3)
                            else:
                                act.wait_ge(raw_in[w], 16 * n + {"v": 32, "o": 16, "k": 48}[w])
                            used, count = {"v": (v_filled, 4 * n + 4), "o": (out_filled, 8 * n + 4 + OUT_FILLED_CREDIT),
                                           "q": (qk_filled, 8 * n + 14), "k": (qk_filled, 8 * n + 16)}[w]
                            act.wait_ge(used, count)
                            act.activation(weight_view(w_hi[w], w), raw_view(w), ACT.Copy).then_inc(w_hi_done, 1)
                    for step, ahead, h, kind, half in QK_SPLITS:
                        if step == s:
                            qk_high(n + ahead, h, kind, half, NCHUNK * n + (NCHUNK // 2 if ahead else 1))
                    if s == 2:
                        v_high(n, 0, p_turned, NCHUNK * n + 1 + P_TURNED_CREDIT)
                    if s == 5:
                        v_high(n, 1, pv_done, 4 * n + 1)

            act.sem_inc(exp_done, EXP_DONE_CREDIT)
            for n, w in enumerate(W_FIRST):
                if n == 3:
                    for idx in range(4):
                        v_copy(0, idx)
                    for j in range(4):
                        qk_high(0, 0, j % 2, j // 2, None)
                    act.wait_ge(qk_filled, 8)
                if w == "q":
                    act.wait_ge(q_scaled, 1 + n // 3)
                else:
                    act.wait_ge(raw_in[w], 16 + 16 * (n // 3))
                act.activation(weight_view(w_hi[w], w), raw_view(w), ACT.Copy).then_inc(w_hi_done, 1)
            exps(0, 0, False)
            batches(act, body)
            ctx_high(NPAIR, 0)

        @block.vector
        def _(dve):
            def scale_q(m):
                dve.wait_ge(raw_in["q"], 16 * (m + 1))
                dve.tensor_scalar(raw["q"][:, :, :], raw["q"][:, :, :], float(1.0 / np.sqrt(HD)), None,
                                  ALU.mult).then_inc(q_scaled, 1)

            def products(m, idx):
                kind, t = QK_ORDER[idx]
                pair = ps_f[:, bank(kind, t, m)].rearrange("p (a n) -> p a n", a=2)
                dve.wait_ge(qk_filled, 8 * m + idx + 1)
                before = 8 * m + idx - 1
                if not (isinstance(before, int) and before <= 0):
                    dve.wait_ge(rot_done, before)
                dve.tensor_tensor(prod_a[:, idx % 2], pair, cs[:, t], ALU.mult)
                dve.tensor_tensor(prod_b[:, idx % 2], pair, cs[:, t, ::-1], ALU.mult).then_inc(prod_done, 1)

            parts = [0]
            for s in range(STEPS):
                i = s % NT
                parts.append(parts[-1] + (1 if i == 0 else 2 if i <= 4 else 3))

            def part_maxima(n, s, which):
                i = s % NT
                ci, c, k = chunks(s)[which]
                at = which
                dve.wait_ge(scored, NCHUNK * n + ci + 1)
                if c == i // 4:
                    dve.sem_inc(dve_own, 1)
                    own = ps_s[:, ci % 3, k - P:k]
                    dve.tensor_tensor_reduce(own, own, msk[:, :], 1.0, -3e38, ALU.add, ALU.max,
                                             part_max[:, s % 2, at:at + 1]).then_inc(part_done, 1)
                    at += 1
                    k -= P
                if k:
                    dve.tensor_reduce(part_max[:, s % 2, at:at + 1], ps_s[:, ci % 3, 0:k], AX.X, ALU.max)\
                       .then_inc(part_done, 1)
                    at += 1
                if c == i // 4:
                    dve.wait_ge(part_done, (parts[STEPS] * n if not isinstance(n, int) else 0) + parts[s] + at)
                    dve.tensor_reduce(neg_max[:, s % 4:s % 4 + 1], part_max[:, s % 2, 0:at], AX.X, ALU.max,
                                      negate=True).then_inc(max_done, 1)

            def pt_low(n, s, ci, c, k):
                i = s % NT
                at = (slice(4 * c, 4 * c + k // P), slice(P * (i % 4), P * (i % 4) + P))
                dve.wait_ge(pt_hi_done, NCHUNK * n + ci + 1)
                dve.tensor_tensor(pt_lo[i // 4][:, at[0], at[1]], ps_t[:, ci % 2, 0:k].rearrange("p (j q) -> p j q", q=P),
                                  f(pt_hi[i // 4][:, at[0], at[1]]), ALU.subtract).then_inc(pt_lo_done, 1)

            def ctx_low(n, k):
                dve.wait_ge(ctx_hi_done, 4 * n + k + 1)
                dve.tensor_tensor(ctx_lo[:, :], ps_c[:, :], f(ctx_hi[:, :]), ALU.subtract).then_inc(ctx_lo_done, 1)

            def reciprocal(n, r):
                h, c = divmod(r, 2)
                blocks = slice(4 * c, 4 * c + 4)
                dve.wait_ge(exp_done, NCHUNK * n + chunks(NT * h + 4 * c + 3)[-1][0] + 1 + EXP_DONE_CREDIT)
                if c:
                    dve.tensor_tensor(den_sum[:, h, blocks], den[:, h, blocks, 0], den[:, h, blocks, 1],
                                      ALU.add).then_inc(den_summed, 1)
                    dve.wait_ge(den_summed, 2 * n + h + 1)
                    dve.reciprocal(rden[:, h, blocks], den_sum[:, h, blocks]).then_inc(rden_done, 1)
                else:
                    dve.reciprocal(rden[:, h, blocks], den[:, h, blocks, 0]).then_inc(rden_done, 1)

            def add_out(n, w, kind):
                h = 1 if w < 4 else 0
                dve.wait_ge(out_filled, 8 * n + w + 1 + OUT_FILLED_CREDIT)
                for u in range(2):
                    t = 4 * (w // 2 % 2) + 2 * (w % 2) + u
                    last = dve.scalar_tensor_tensor(out=x[:, t], in0=ps_f[:, bank("o", w, n), D * u:D * u + D],
                                                    scalar=rden[:, h, t:t + 1], in1=x[:, t], op0=ALU.mult, op1=ALU.add)
                last.then_inc(out_added, 1)

            def body(n, b, kind_of_body):
                for s in range(STEPS):
                    m, nxt = (n, s + 1) if s + 1 < STEPS else (n + 1, 0)
                    if s == 7:
                        scale_q(n + 2)
                    part_maxima(m, nxt, 0)
                    if s in QKV_FILLS and QKV_FILLS[s][0] != "v":
                        products(n + 1, QK_ORDER.index(QKV_FILLS[s]))
                    work = chunks(s)
                    pt_low(n, s, *work[0])
                    if len(chunks(nxt)) > 1:
                        part_maxima(m, nxt, 1)
                    if len(work) > 1:
                        pt_low(n, s, *work[1])
                    if s in OUT_FILLS:
                        w = OUT_FILLS[s]
                        if w % 2 == 0:
                            dve.wait_ge(rden_done, 4 * n + w // 2 - 1 + RDEN_BEFORE)
                        if kind_of_body == "first" and w in (4, 6):
                            dve.wait_ge(x_in[w // 2 - 2], 16 * b + 16)
                        add_out(n, w, kind_of_body)
                    if s in (4, 8, 12, 15):
                        reciprocal(n, {4: 0, 8: 1, 12: 2, 15: 3}[s])
                    if s % 4 == 3:
                        ctx_low(n, s // 4)

            for t in (pt_lo[1][:, :, :], v_hi[:, :, HD:], ctx_hi[:, :], ctx_lo[:, :], w_hi["o"][:, :, :], w_lo["o"][:, :, :]):
                dve.memset(f(t), 0.0).then_inc(zeroed, 1)
            dve.memset(x[:, :, :], 0.0).then_inc(zeroed, 1)
            dve.memset(rden[:, :, :], 0.0).then_inc(rden_done, RDEN_BEFORE)
            dve.sem_inc(pt_lo_done, PT_LO_DONE_CREDIT)
            dve.sem_inc(ctx_lo_done, CTX_LO_DONE_CREDIT)
            dve.sem_inc(out_added, OUT_ADDED_CREDIT)
            scale_q(0)
            dve.wait_ge(const_in, 48)
            for idx in range(8):
                products(0, idx)
            scale_q(1)
            part_maxima(0, 0, 0)
            batches(dve, body)
            add_out(NPAIR, 0, None)
            add_out(NPAIR, 1, None)
            ctx_low(NPAIR, 0)
            add_out(NPAIR, 2, None)
            add_out(NPAIR, 3, None)

        @block.tensor
        def _(pe):
            def bank_free(n, kind, idx):
                at = FILLS.index((kind, idx)) - 2
                before, j = FILLS[at]
                back = 1 if at < 0 else 0
                if before == "o":
                    pe.wait_ge(out_added, 8 * (n - back) + j + 1 + OUT_ADDED_CREDIT)
                elif before == "v":
                    pe.wait_ge(v_raw_done, 4 * (n + 1 - back) + j + 1)
                else:
                    pe.wait_ge(prod_done, 8 * (n + 1 - back) + QK_ORDER.index((before, j)) + 1)

            def fill(m, kind, idx):
                out = ps_f[:, bank(kind, idx, m)]
                if kind == "v":
                    for u in range(2):
                        t = 2 * idx + u
                        n = 0
                        for kt in range(KT):
                            cols = slice(P * t, P * t + P)
                            for a, w in passes(xt_hi[:, kt, cols], xt_lo[:, kt, cols], w_hi["v"][:, kt], w_lo["v"][:, kt]):
                                last = pe.matmul(out[:, 256 * u:256 * u + 256], a, w, start=n == 0, stop=n == 5)
                                n += 1
                    last.then_inc(v_filled, 1)
                    return
                for two in range(2):
                    n = 0
                    for kt in range(KT):
                        cols, toks = slice(P * two, P * two + P), slice(256 * idx, 256 * idx + 256)
                        for w, a in passes(w_hi[kind][:, kt, cols], w_lo[kind][:, kt, cols], xt_hi[:, kt, toks], xt_lo[:, kt, toks]):
                            last = pe.matmul(out[:, 256 * two:256 * two + 256], w, a, start=n == 0, stop=n == 5)
                            n += 1
                last.then_inc(qk_filled, 1)

            def fill_out(w):
                h = 1 if w < 4 else 0
                for u in range(2):
                    cols = slice(P * (2 * (w % 2) + u), P * (2 * (w % 2) + u) + P)
                    n = 0
                    for a, ww in passes(ctx_hi[:, cols], ctx_lo[:, cols], w_hi["o"][:, h], w_lo["o"][:, h]):
                        last = pe.matmul(ps_f[:, bank("o", w, None), D * u:D * u + D], a, ww, start=n == 0, stop=n == 2)
                        n += 1
                last.then_inc(out_filled, 1)

            def scores(n, s, which):
                h, i = divmod(s, NT)
                ci, c, k = chunks(s)[which]
                pe.wait_ge(exp_done, NCHUNK * n + ci - 2 + EXP_DONE_CREDIT)
                j = 0
                for q, kk in passes(qk_hi[:, 0, h, P * i:P * i + P], qk_lo[:, 0, h, P * i:P * i + P],
                                    qk_hi[:, 1, h, CH * c:CH * c + k], qk_lo[:, 1, h, CH * c:CH * c + k]):
                    last = pe.matmul(ps_s[:, ci % 3, 0:k], q, kk, start=j == 0, stop=j == 2)
                    j += 1
                last.then_inc(scored, 1)

            def turn(n, s, which):
                ci, c, k = chunks(s)[which]
                pe.wait_ge(exp_done, NCHUNK * n + ci + 1 + EXP_DONE_CREDIT)
                pe.wait_ge(pt_lo_done, NCHUNK * n + ci - 1 + PT_LO_DONE_CREDIT)
                for j in range(k // P):
                    last = pe.transpose(ps_t[:, ci % 2, P * j:P * j + P], probs[:, s % 2, CH * c + P * j:CH * c + P * j + P], idn[:, :])
                last.then_inc(p_turned, 1)

            def context(h, c, blocks):
                final = 4 * c + 3
                for j in blocks:
                    first = max(0, P * (j - 4 * c))
                    v = (v_hi[:, j, HD * h:HD * h + HD], v_lo[:, j, HD * h:HD * h + HD])
                    p_ = (pt_hi[c][:, j, first:], pt_lo[c][:, j, first:])
                    for m, (a, b) in enumerate(passes(*v, *p_)):
                        last = pe.matmul(ps_c[:, first:], a, b, start=j == 0 and m == 0, stop=j == final and m == 2)
                if final in blocks:
                    last.then_inc(pv_done, 1)

            def add_context(n, h, i):
                if i == 0:
                    pe.wait_ge(ctx_lo_done, 4 * n + 2 * h + CTX_LO_DONE_CREDIT)
                    pe.wait_ge(pt_lo_done, NCHUNK * n + 12 * h + PT_LO_DONE_CREDIT)
                if i == 4:
                    pe.wait_ge(ctx_lo_done, 4 * n + 2 * h + 1 + CTX_LO_DONE_CREDIT)
                    pe.wait_ge(pt_lo_done, NCHUNK * n + 12 * h + 4 + PT_LO_DONE_CREDIT)
                    pe.wait_ge(v_lo_done, 2 * n + h + 1)
                if i < 4:
                    context(1 - h, 1, (2 * i, 2 * i + 1))
                else:
                    context(h, 0, (i - 4,))

            def body(n, b, kind_of_body):
                for s in range(STEPS):
                    h, i = divmod(s, NT)
                    m, nxt = (n, s + 1) if s + 1 < STEPS else (n + 1, 0)
                    if s == 3:
                        pe.wait_ge(qk_lo_done, QK_BEFORE + 8 * n)
                    if s in (7, 11):
                        pe.wait_ge(qk_lo_done, QK_BEFORE + 8 * n + (2 if s == 7 else 4))
                    if s == STEPS - 1:
                        pe.wait_ge(qk_lo_done, QK_BEFORE + 8 * n + 6)
                    scores(m, nxt, 0)
                    if s in QKV_FILLS:
                        kind, idx = QKV_FILLS[s]
                        if kind == "q" and idx in (0, 2) and kind_of_body == "last":
                            pe.wait_ge(xt_in[idx // 2], 32 * b + 64)
                        if idx == 0:
                            pe.wait_ge(w_lo_done, {"q": 4 * n + 4, "k": 4 * n + 5, "v": W_BEFORE + 4 * n + 1}[kind])
                        bank_free(n, kind, idx)
                        fill(n + 1, kind, idx)
                    if i % 4:
                        add_context(n, h, i)
                    turn(n, s, 0)
                    if len(chunks(nxt)) > 1:
                        scores(m, nxt, 1)
                    if s in OUT_FILLS:
                        w = OUT_FILLS[s]
                        if w % 2 == 0:
                            pe.wait_ge(ctx_lo_done, 4 * n + w // 2 + CTX_LO_DONE_CREDIT)
                        if w == 4:
                            pe.wait_ge(w_lo_done, W_BEFORE + 4 * n + W_INDEX["o"] + 1)
                        bank_free(n, "o", w)
                        fill_out(w)
                    if len(chunks(s)) > 1:
                        turn(n, s, 1)
                    if i % 4 == 0:
                        add_context(n, h, i)

            pe.sem_inc(out_filled, OUT_FILLED_CREDIT)
            pe.sem_inc(p_turned, P_TURNED_CREDIT)
            for half in range(2):
                pe.wait_ge(xt_in[half], 32)
            order = QKV_ORDER
            for at, (kind, idx) in enumerate(order):
                if idx == 0:
                    pe.wait_ge(w_lo_done, "qkv".index(kind) + 1)
                if at >= 2:
                    before, j = order[at - 2]
                    if before == "v":
                        pe.wait_ge(v_raw_done, j + 1)
                    else:
                        pe.wait_ge(prod_done, QK_ORDER.index((before, j)) + 1)
                fill(0, kind, idx)
            pe.wait_ge(const_in, 48)
            pe.wait_ge(qk_lo_done, 2)
            scores(0, 0, 0)
            pe.wait_ge(v_raw_done, 4)
            pe.wait_ge(zeroed, 9)
            batches(pe, body)
            n = NPAIR
            for w in range(2):
                pe.wait_ge(ctx_lo_done, 4 * n + CTX_LO_DONE_CREDIT)
                bank_free(n, "o", w)
                fill_out(w)
            pe.wait_ge(pt_lo_done, NCHUNK * n + PT_LO_DONE_CREDIT)
            context(1, 1, range(8))
            for w in range(2, 4):
                pe.wait_ge(ctx_lo_done, 4 * n + 1 + CTX_LO_DONE_CREDIT)
                pe.wait_ge(out_added, 8 * n + w + OUT_ADDED_CREDIT)
                fill_out(w)


def constants():
    freqs = 1.0 / 10000.0 ** (np.arange(0, HD, 2, dtype=np.float32) / HD)
    ang = np.outer(np.arange(S, dtype=np.float32), freqs)
    table = np.stack([np.cos(ang), np.sin(ang)]).transpose(2, 0, 1)
    table = table.reshape(HALF, 2, 4, 256).transpose(0, 2, 1, 3)
    return {
        "rope": np.ascontiguousarray(np.concatenate([table, table]), dtype=np.float32),
        "mask": np.triu(np.full((P, P), NEG, np.float32), 1),
        "ident": np.eye(P, dtype=np.float32),
    }


_INS = ['L0_attn_x', 'L0_attn_Wq', 'L0_attn_Wk', 'L0_attn_Wv', 'L0_attn_Wo', 'L0_ffn_gate_up_proj', 'L0_ffn_down_proj']


def macaron(nc, x, wq, wk, wv, wo, gate_up, down, rope, mask, ident, out):
    x1 = nc.dram_tensor("x1", [B, S, D], F32).ap()
    x2 = nc.dram_tensor("x2", [B, S, D], F32).ap()
    xnt = nc.dram_tensor("xnt", [B, 2, P, KT * S], F32).ap().rearrange("b h p (k t) -> b h p k t", k=KT)
    ffn_stage(nc, "ffn1_", x, x1, gate_up, down, ident, xnt)
    attention_stage(nc, x1, x2, xnt, wq, wk, wv, wo, rope, mask, ident)
    ffn_stage(nc, "ffn2_", x2, out, gate_up, down, ident, None)


def kernel(**inputs):
    import numpy as _np
    import concourse.bacc as _bacc
    from concourse import mybir as _mybir
    from concourse.bass_utils import run_bass_kernel_spmd as _run

    nc = _bacc.Bacc("TRN2", target_bir_lowering=False, num_devices=1)
    arrays, args = {}, []
    for name, value in [(name, inputs[name]) for name in _INS] + list(constants().items()):
        a = _np.ascontiguousarray(value)
        arrays[f"in_{name}_dram"] = a
        args.append(nc.dram_tensor(f"in_{name}_dram", a.shape, _mybir.dt.from_np(a.dtype), kind="ExternalInput").ap())
    args.append(nc.dram_tensor("out_0_dram", (B, S, D), F32, kind="ExternalOutput").ap())
    macaron(nc, *args)
    r = _run(nc, [arrays], core_ids=[0])
    return r.results[0]["out_0_dram"]
```

```python
from contextlib import ExitStack

import concourse.bass as bass
import numpy as np
from concourse import mybir

ALU = mybir.AluOpType
ACT = mybir.ActivationFunctionType
AX = mybir.AxisListType
F32 = mybir.dt.float32
F32R = mybir.dt.float32r

P = 128
B, S, D = 4, 1024, 256
H, HD = 16, 128
E, I = 4, 256
EPS = 1e-5
NEG = -1e30
KT = D // P
CH = 512
NCH = S // CH
NT = S // P
PAIRS = H // 2
NPAIR = B * PAIRS
HALF = HD // 2


CTX_LO_DONE_CREDIT = 1
EXP_DONE_CREDIT = 3
INNER_DONE_CREDIT = 2
INNER_LO_CREDIT = 2
OUT_ADDED_CREDIT = 1
OUT_FILLED_CREDIT = 1
P_TURNED_CREDIT = 3
PT_LO_DONE_CREDIT = 2
STORED_CREDIT = 16
XNT_STORED_CREDIT = 32
Y_ADDED_CREDIT = 2
Y_DONE_CREDIT = 2


def passes(hi_a, lo_a, hi_b, lo_b):
    return (hi_a, hi_b), (hi_a, lo_b), (lo_a, hi_b)


def f(ap):
    return ap.bitcast(F32)


def ffn_stage(nc, tag, src, dst, gate_up, down, ident, xnt):
    post = xnt is not None
    with ExitStack() as ctx:
        def sb(name, shape, dt=F32):
            return ctx.enter_context(nc.sbuf_tensor(tag + name, shape, dt))

        def ps(name, shape):
            return ctx.enter_context(nc.psum_tensor(tag + name, shape, F32))

        def signal(name):
            return ctx.enter_context(nc.semaphore(tag + name))

        gu_raw = sb("gu_raw", [P, E, KT, 2 * I])
        gu_hi = sb("gu_hi", [P, E, KT, 2 * I], F32R)
        gu_lo = sb("gu_lo", [P, E, KT, 2 * I], F32R)
        dn_raw = sb("dn_raw", [P, E, KT, D])
        dn_hi = sb("dn_hi", [P, E, KT, D], F32R)
        dn_lo = sb("dn_lo", [P, E, KT, D], F32R)
        idn = sb("idn", [P, P])
        x_in = sb("x_in", [P, NCH, E, D])
        xn = sb("xn", [P, NCH, E, D])
        xt_hi = sb("xt_hi", [P, KT, E, NCH, P], F32R)
        xt_lo = sb("xt_lo", [P, KT, E, NCH, P], F32R)
        x_out = sb("x_out", [P, NCH, E, D])
        xn_out = sb("xn_out", [P, NCH, E, D])
        xo_hi = sb("xo_hi", [P, KT, S], F32R)
        xo_lo = sb("xo_lo", [P, KT, S], F32R)
        mhalf = sb("mhalf", [P, E])
        stats = sb("stats", [P, NCH, E, 6])
        mv = sb("mv", [P, NCH, E, 2])
        var = sb("var", [P, NCH, E])
        minus_mean = sb("minus_mean", [P, NCH, E])
        rstd = sb("rstd", [P, NCH, E])
        shift_in = sb("shift_in", [P, NCH, E])
        o_stats = sb("o_stats", [P, 2, NCH, 6])
        o_mv = sb("o_mv", [P, 2, NCH, 2])
        o_var = sb("o_var", [P, 2, NCH])
        o_minus_mean = sb("o_minus_mean", [P, 2, NCH])
        o_rstd = sb("o_rstd", [P, 2, NCH])
        o_shift = sb("o_shift", [P, 2, NCH])
        sig = sb("sig", [P, 2, CH])
        silu_g = sb("silu_g", [P, 2, CH])
        inner = sb("inner", [P, 2, CH])
        in_hi = sb("in_hi", [P, 2, 2, D], F32R)
        in_lo = sb("in_lo", [P, 2, 2, D], F32R)
        ps_t = ps("ps_t", [P, 2, CH])
        ps_g = ps("ps_g", [P, 2, CH])
        ps_u = ps("ps_u", [P, 2, CH])
        ps_y = ps("ps_y", [P, 2, CH])

        w_in = [signal(f"w_in{e}") for e in range(E)]
        id_in = signal("id_in")
        gu_hi_done = signal("gu_hi_done")
        dn_hi_done = signal("dn_hi_done")
        gu_lo_done = signal("gu_lo_done")
        dn_lo_done = signal("dn_lo_done")
        x_loaded = [signal(f"x_loaded{c}") for c in range(NCH)]
        half_set = signal("half_set")
        stats_done = signal("stats_done")
        mv_done = signal("mv_done")
        var_done = signal("var_done")
        rstd_step = signal("rstd_step")
        shift_done = signal("shift_done")
        xn_done = signal("xn_done")
        res_in = [signal(f"res_in{e}") for e in range(E)]
        xt_turned = signal("xt_turned")
        xt_hi_done = signal("xt_hi_done")
        xt_lo_done = signal("xt_lo_done")
        xo_turned = signal("xo_turned")
        xo_hi_done = signal("xo_hi_done")
        xo_lo_done = signal("xo_lo_done")
        gu_done = signal("gu_done")
        sigmoid_done = signal("sigmoid_done")
        silu_step = signal("silu_step")
        inner_done = signal("inner_done")
        inner_hi = signal("inner_hi")
        inner_lo = signal("inner_lo")
        y_done = signal("y_done")
        y_added = signal("y_added")
        o_stats_done = signal("o_stats_done")
        o_mv_done = signal("o_mv_done")
        o_var_done = signal("o_var_done")
        o_rstd_step = signal("o_rstd_step")
        o_shift_done = signal("o_shift_done")
        xn_out_done = signal("xn_out_done")
        stored = signal("stored")
        xnt_stored = signal("xnt_stored")
        sp_own = signal("sp_own")
        dve_own = signal("dve_own")

        IN_BANKS = [(0, 0), (1, 0), (0, 2), (1, 2)]
        OUT_BANKS = [(0, 0), (0, 1), (1, 0), (1, 1)]

        def xt_part(t, j):
            kt, e = IN_BANKS[j]
            return t[:, kt, e:e + 2].rearrange("p e c q -> p (e c q)")

        def xo_part(t, j):
            kt, c = OUT_BANKS[j]
            return t[:, kt, CH * c:CH * c + CH].rearrange("p (q e) -> p e q", e=E)

        def batches(eng, body):
            body(0)
            with eng.Fori(1, B - 1) as k:
                body(k)
            body(B - 1)

        def is_first(k):
            return isinstance(k, int) and k == 0

        def is_last(k):
            return isinstance(k, int) and k == B - 1

        block = ctx.enter_context(nc.Block())

        @block.sync
        def _(sp):
            def by_token(t, b):
                return t[b].rearrange("(c p e) d -> p c e d", c=NCH, e=E)

            def load_input(b, c):
                sp.dma_start(x_in[:, c], by_token(src, b)[:, c]).then_inc(x_loaded[c], 16)

            def load_residual(b, e):
                sp.dma_start(x_out[:, :, e], by_token(src, b)[:, :, e]).then_inc(res_in[e], 16)

            if post:
                sp.sem_inc(xnt_stored, XNT_STORED_CREDIT)
            for c in range(NCH):
                load_input(0, c)
            sp.dma_start(idn[:, :], ident).then_inc(id_in, 16)
            for e in range(E):
                sp.dma_start(gu_raw[:, e], gate_up[e].rearrange("(k p) n -> p k n", p=P)).then_inc(w_in[e], 16)
                sp.dma_start(dn_raw[:, e], down[e].rearrange("(k p) n -> p k n", p=P)).then_inc(w_in[e], 16)
            for e in range(E):
                load_residual(0, e)
            for n in range(2 * NCH):
                sp.wait_ge(xn_done, n + 1)
                load_input(1 + n // NCH, n % NCH)

            def body(k):
                def next_input(c):
                    if not is_last(k):
                        sp.wait_ge(xn_done, 2 * k + 5 + c)
                        sp.sem_inc(sp_own, 1)
                        load_input((k + 3) % B, c)

                for e in range(E):
                    n = E * k + e
                    if post and e == 2 and not is_first(k):
                        sp.wait_ge(xo_lo_done, 4 * k)
                        sp.sem_inc(sp_own, 1)
                        sp.dma_start(xnt[k - 1, 0], f(xo_hi[:, :, :])).then_inc(xnt_stored, 16)
                        sp.dma_start(xnt[k - 1, 1], f(xo_lo[:, :, :])).then_inc(xnt_stored, 16)
                    if e == E - 1:
                        next_input(0)
                    sp.wait_ge(y_added, n + 1)
                    sp.sem_inc(sp_own, 1)
                    sp.dma_start(by_token(dst, k)[:, :, e], x_out[:, :, e]).then_inc(stored, 16)
                    if e == E - 1:
                        next_input(1)
                    if not is_last(k):
                        sp.wait_ge(stored, 16 * n + 16)
                        if post:
                            sp.wait_ge(xn_out_done, n + 1)
                        sp.sem_inc(sp_own, 1)
                        load_residual(k + 1, e)

            batches(sp, body)
            sp.wait_ge(stored, 16 * B * E)
            for c in range(NCH):
                sp.wait_ge(x_loaded[c], 16 * (B + 2))
            if post:
                sp.wait_ge(xo_lo_done, 4 * B)
                sp.dma_start(xnt[B - 1, 0], f(xo_hi[:, :, :])).then_inc(xnt_stored, 16)
                sp.dma_start(xnt[B - 1, 1], f(xo_lo[:, :, :])).then_inc(xnt_stored, 16)
                sp.wait_ge(xnt_stored, 32 * B + XNT_STORED_CREDIT)

        @block.gpsimd
        def _(pool):
            pool.sem_inc(inner_lo, INNER_LO_CREDIT)
            pool.memset(mhalf[:, :], -0.5).then_inc(half_set, 1)
            pool.wait_ge(half_set, 1)

            def root(n, c):
                pool.wait_ge(var_done, 2 * n + c + 1)
                pool.tensor_tensor(rstd[:, c], var[:, c], mhalf[:, :], ALU.pow).then_inc(rstd_step, 1)
                pool.wait_ge(rstd_step, 2 * n + c + 1)
                pool.tensor_tensor(shift_in[:, c], minus_mean[:, c], rstd[:, c], ALU.mult).then_inc(shift_done, 1)

            def root_out(n, e):
                pool.wait_ge(o_var_done, n + 1)
                if not (isinstance(n, int) and n < 2):
                    pool.wait_ge(xn_out_done, n - 1)
                pool.tensor_tensor(o_rstd[:, e % 2], o_var[:, e % 2], mhalf[:, 0:NCH], ALU.pow).then_inc(o_rstd_step, 1)
                pool.wait_ge(o_rstd_step, n + 1)
                pool.tensor_tensor(o_shift[:, e % 2], o_minus_mean[:, e % 2], o_rstd[:, e % 2], ALU.mult).then_inc(o_shift_done, 1)

            def inner_low(n, e):
                pool.wait_ge(inner_hi, n + 1)
                pool.wait_ge(y_done, n - 1 + Y_DONE_CREDIT)
                pool.tensor_tensor(in_lo[:, e % 2].rearrange("p a b -> p (a b)"), inner[:, e % 2],
                                   f(in_hi[:, e % 2].rearrange("p a b -> p (a b)")), ALU.subtract).then_inc(inner_lo, 1)

            def split_down(e):
                pool.wait_ge(dn_hi_done, e + 1)
                pool.tensor_tensor(dn_lo[:, e], dn_raw[:, e], f(dn_hi[:, e]), ALU.subtract).then_inc(dn_lo_done, 1)

            def body(k):
                for e in range(E):
                    if post and not (is_first(k) and e == 0):
                        root_out(E * k + e - 1, (e - 1) % E)
                    if not (is_last(k) and e == E - 1):
                        inner_low(E * k + e + 1, (e + 1) % E)
                    if e in (0, 2) and not is_last(k):
                        root(k + 2, e // 2)

            for c in range(NCH):
                root(0, c)
            for e in range(3):
                split_down(e)
            inner_low(0, 0)
            for c in range(NCH):
                root(1, c)
            split_down(3)
            batches(pool, body)
            if post:
                root_out(E * B - 1, E - 1)

        @block.scalar
        def _(act):
            def split_gate_up(e):
                act.wait_ge(w_in[e], 32)
                act.activation(gu_hi[:, e], gu_raw[:, e], ACT.Copy).then_inc(gu_hi_done, 1)

            def split_down(e):
                act.activation(dn_hi[:, e], dn_raw[:, e], ACT.Copy).then_inc(dn_hi_done, 1)

            def normalise(n, c, used):
                act.wait_ge(shift_done, 2 * n + c + 1)
                if used is not None:
                    act.wait_ge(xt_turned, used)
                for e in range(E):
                    last = act.activation(xn[:, c, e], x_in[:, c, e], ACT.Identity, bias=shift_in[:, c, e:e + 1],
                                          scale=rstd[:, c, e:e + 1])
                last.then_inc(xn_done, 1)

            def normalise_out(n, e):
                act.wait_ge(o_shift_done, n + 1)
                for c in range(NCH):
                    last = act.activation(xn_out[:, c, e], x_out[:, c, e], ACT.Identity, bias=o_shift[:, e % 2, c:c + 1],
                                          scale=o_rstd[:, e % 2, c:c + 1])
                last.then_inc(xn_out_done, 1)

            def turn_in_hi(n, js):
                for j in js:
                    act.wait_ge(xt_turned, 4 * n + j + 1)
                    act.activation(xt_part(xt_hi, j), ps_t[:, j % 2], ACT.Copy).then_inc(xt_hi_done, 1)

            def turn_out_hi(k):
                for j in range(4):
                    act.wait_ge(xo_turned, 4 * k - 3 + j)
                    act.activation(xo_part(xo_hi, j), ps_t[:, j % 2], ACT.Copy).then_inc(xo_hi_done, 1)

            def sigmoid(n, e):
                act.wait_ge(gu_done, n + 1)
                act.wait_ge(inner_done, n - 1 + INNER_DONE_CREDIT)
                act.activation(sig[:, e % 2], ps_g[:, e % 2], ACT.Sigmoid).then_inc(sigmoid_done, 1)

            def inner_high(n, e):
                act.wait_ge(y_done, n - 1 + Y_DONE_CREDIT)
                act.wait_ge(inner_done, n + 1 + INNER_DONE_CREDIT)
                act.activation(in_hi[:, e % 2].rearrange("p a b -> p (a b)"), inner[:, e % 2],
                               ACT.Copy).then_inc(inner_hi, 1)

            def body(k):
                for e in range(E):
                    n = E * k + e
                    more = not (is_last(k) and e == E - 1)
                    if more:
                        sigmoid(n + 1, (e + 1) % E)
                    if post and e != 1 and not (is_first(k) and e == 0):
                        normalise_out(n - 1, (e - 1) % E)
                    if e in (0, 2) and not is_last(k):
                        act.wait_ge(gu_done, E * k + e + 2)
                        turn_in_hi(k + 1, (e, e + 1))
                    if more:
                        inner_high(n + 1, (e + 1) % E)
                    if post and e == 1:
                        if not is_first(k):
                            act.wait_ge(xnt_stored, 32 * k - 32 + XNT_STORED_CREDIT)
                            turn_out_hi(k)
                        normalise_out(n - 1, 0)
                    if e >= 2 and not is_last(k):
                        normalise(k + 2, e - 2, 4 * k + 8)

            split_gate_up(0)
            split_down(0)
            split_gate_up(1)
            for c in range(NCH):
                normalise(0, c, None)
            split_gate_up(2)
            turn_in_hi(0, range(4))
            split_gate_up(3)
            split_down(1)
            sigmoid(0, 0)
            split_down(2)
            inner_high(0, 0)
            split_down(3)
            for c in range(NCH):
                normalise(1, c, 4)
            batches(act, body)
            if post:
                normalise_out(E * B - 1, E - 1)
                act.wait_ge(xnt_stored, 32 * (B - 1) + XNT_STORED_CREDIT)
                turn_out_hi(B)

        @block.vector
        def _(dve):
            dve.sem_inc(inner_done, INNER_DONE_CREDIT)

            def input_stats(n, c):
                for e in range(E):
                    last = dve.bn_stats(stats[:, c, e], x_in[:, c, e])
                last.then_inc(stats_done, 1)

            def input_mean_var(n, c):
                dve.wait_ge(stats_done, 2 * n + c + 1)
                dve.sem_inc(dve_own, 1)
                for e in range(E):
                    last = dve.bn_aggr(mv[:, c, e], stats[:, c, e])
                last.then_inc(mv_done, 1)

            def input_moments(n, c):
                dve.wait_ge(mv_done, 2 * n + c + 1)
                dve.tensor_scalar(minus_mean[:, c], mv[:, c, :, 0], -1.0, None, ALU.mult)
                dve.tensor_scalar(var[:, c], mv[:, c, :, 1], EPS, None, ALU.add).then_inc(var_done, 1)

            def result_stats(n, e):
                dve.wait_ge(y_added, n + 1)
                dve.sem_inc(dve_own, 1)
                for c in range(NCH):
                    last = dve.bn_stats(o_stats[:, e % 2, c], x_out[:, c, e])
                last.then_inc(o_stats_done, 1)

            def result_mean_var(n, e):
                dve.wait_ge(o_stats_done, n + 1)
                dve.sem_inc(dve_own, 1)
                for c in range(NCH):
                    last = dve.bn_aggr(o_mv[:, e % 2, c], o_stats[:, e % 2, c])
                last.then_inc(o_mv_done, 1)

            def result_moments(n, e):
                dve.wait_ge(o_mv_done, n + 1)
                if not (isinstance(n, int) and n < 2):
                    dve.wait_ge(o_shift_done, n - 1)
                    dve.sem_inc(dve_own, 1)
                dve.tensor_scalar(o_minus_mean[:, e % 2], o_mv[:, e % 2, :, 0], -1.0, None, ALU.mult)
                dve.tensor_scalar(o_var[:, e % 2], o_mv[:, e % 2, :, 1], EPS, None, ALU.add).then_inc(o_var_done, 1)

            def turn_in_lo(n, js):
                for j in js:
                    dve.wait_ge(xt_hi_done, 4 * n + j + 1)
                    dve.tensor_tensor(xt_part(xt_lo, j), ps_t[:, j % 2], f(xt_part(xt_hi, j)),
                                      ALU.subtract).then_inc(xt_lo_done, 1)

            def turn_out_lo(k):
                for j in range(4):
                    dve.wait_ge(xo_hi_done, 4 * k - 3 + j)
                    dve.tensor_tensor(xo_part(xo_lo, j), ps_t[:, j % 2].rearrange("p (e q) -> p e q", q=P),
                                      f(xo_part(xo_hi, j)), ALU.subtract).then_inc(xo_lo_done, 1)

            def silu(n, e):
                dve.wait_ge(sigmoid_done, n + 1)
                dve.tensor_tensor(silu_g[:, e % 2], ps_g[:, e % 2], sig[:, e % 2], ALU.mult).then_inc(silu_step, 1)

            def make_inner(n, e):
                dve.wait_ge(silu_step, n + 1)
                dve.wait_ge(inner_lo, n - 1 + INNER_LO_CREDIT)
                dve.tensor_tensor(inner[:, e % 2], ps_u[:, e % 2], silu_g[:, e % 2], ALU.mult).then_inc(inner_done, 1)

            def add_y(n, k, e):
                dve.wait_ge(res_in[e], 16 * k + 16)
                dve.wait_ge(y_done, n + 1 + Y_DONE_CREDIT)
                dve.scalar_tensor_tensor(out=x_out[:, :, e], in0=ps_y[:, e % 2].rearrange("p (c d) -> p c d", c=NCH),
                                         scalar=0.5, in1=x_out[:, :, e], op0=ALU.mult, op1=ALU.add).then_inc(y_added, 1)

            def split_gate_up(e):
                dve.wait_ge(gu_hi_done, e + 1)
                dve.tensor_tensor(gu_lo[:, e], gu_raw[:, e], f(gu_hi[:, e]), ALU.subtract).then_inc(gu_lo_done, 1)

            def body(k):
                for e in range(E):
                    n = E * k + e
                    more = not (is_last(k) and e == E - 1)
                    before = post and not (is_first(k) and e == 0)
                    if more:
                        silu(n + 1, (e + 1) % E)
                    if before:
                        result_mean_var(n - 1, (e - 1) % E)
                    if more:
                        make_inner(n + 1, (e + 1) % E)
                    if before:
                        result_moments(n - 1, (e - 1) % E)
                    chunk = e // 2 if e in (0, 2) and not is_last(k) else None
                    if chunk is not None:
                        dve.wait_ge(x_loaded[chunk], 16 * k + 48)
                        dve.sem_inc(dve_own, 1)
                        input_stats(k + 2, chunk)
                        turn_in_lo(k + 1, (e,))
                        input_mean_var(k + 2, chunk)
                        turn_in_lo(k + 1, (e + 1,))
                        input_moments(k + 2, chunk)
                    add_y(n, k, e)
                    if post:
                        result_stats(n, e)
                        if e == 1 and not is_first(k):
                            turn_out_lo(k)

            for c in range(NCH):
                dve.wait_ge(x_loaded[c], 16)
                input_stats(0, c)
                input_mean_var(0, c)
                input_moments(0, c)
            for e in range(3):
                split_gate_up(e)
            turn_in_lo(0, range(4))
            split_gate_up(3)
            for c in range(NCH):
                dve.wait_ge(x_loaded[c], 32)
                input_stats(1, c)
                input_mean_var(1, c)
                if c == 0:
                    silu(0, 0)
                dve.wait_ge(shift_done, c + 1)
                input_moments(1, c)
                if c == 0:
                    make_inner(0, 0)
            batches(dve, body)
            if post:
                result_mean_var(E * B - 1, E - 1)
                result_moments(E * B - 1, E - 1)
                turn_out_lo(B)

        @block.tensor
        def _(pe):
            pe.sem_inc(y_done, Y_DONE_CREDIT)

            def turn_in(n, js, freed):
                pe.wait_ge(xn_done, 2 * n + 2)
                for j in js:
                    if freed is not None:
                        pe.wait_ge(freed[0], freed[1] + j % 2)
                    elif j >= 2:
                        pe.wait_ge(xt_lo_done, j - 1)
                    kt, e0 = IN_BANKS[j]
                    for i in range(4):
                        e, c = e0 + i // 2, i % 2
                        last = pe.transpose(ps_t[:, j % 2, P * i:P * i + P], xn[:, c, e, P * kt:P * kt + P], idn[:, :])
                    last.then_inc(xt_turned, 1)

            def turn_out(k, freed):
                pe.wait_ge(xn_out_done, E * k)
                for j in range(4):
                    if j < 2:
                        pe.wait_ge(freed[0], freed[1] + j)
                    else:
                        pe.wait_ge(xo_lo_done, 4 * k - 5 + j)
                    kt, c = OUT_BANKS[j]
                    for e in range(E):
                        last = pe.transpose(ps_t[:, j % 2, P * e:P * e + P], xn_out[:, c, e, P * kt:P * kt + P], idn[:, :])
                    last.then_inc(xo_turned, 1)

            def gate_up_of(n, e, turned_before):
                pe.wait_ge(xt_lo_done, turned_before)
                pe.wait_ge(inner_done, n - 1 + INNER_DONE_CREDIT)
                for out, col in ((ps_g, 0), (ps_u, I)):
                    for m in range(2):
                        j = 0
                        for kt in range(KT):
                            cols = slice(col + P * m, col + P * m + P)
                            x_h = xt_hi[:, kt, e].rearrange("p c q -> p (c q)")
                            x_l = xt_lo[:, kt, e].rearrange("p c q -> p (c q)")
                            for w, x in passes(gu_hi[:, e, kt, cols], gu_lo[:, e, kt, cols], x_h, x_l):
                                last = pe.matmul(out[:, e % 2, D * m:D * m + D], w, x, start=j == 0, stop=j == 3 * KT - 1)
                                j += 1
                last.then_inc(gu_done, 1)

            def down_of(n, e):
                pe.wait_ge(inner_lo, n + 1 + INNER_LO_CREDIT)
                if not (isinstance(n, int) and n < 2):
                    pe.wait_ge(y_added, n - 1)
                for c in range(NCH):
                    j = 0
                    for m in range(2):
                        i_h, i_l = in_hi[:, e % 2, m, P * c:P * c + P], in_lo[:, e % 2, m, P * c:P * c + P]
                        for i, w in passes(i_h, i_l, dn_hi[:, e, m], dn_lo[:, e, m]):
                            last = pe.matmul(ps_y[:, e % 2, D * c:D * c + D], i, w, start=j == 0, stop=j == 5)
                            j += 1
                last.then_inc(y_done, 1)

            def body(k):
                for e in range(E):
                    n = E * k + e
                    if e < 2:
                        if is_first(k):
                            pe.wait_ge(gu_lo_done, e + 3)
                        gate_up_of(n + 2, e + 2, 4 * k + 4)
                    elif not is_last(k):
                        gate_up_of(n + 2, e - 2, 4 * k + 6)
                    if e in (0, 2) and not is_last(k):
                        after_out = post and e == 2 and not is_first(k)
                        turn_in(k + 1, (e, e + 1), (xo_lo_done, 4 * k - 1) if after_out else (xt_lo_done, 4 * k + 3 + e))
                    if is_first(k):
                        pe.wait_ge(dn_lo_done, e + 1)
                    down_of(n, e)
                    if post and e == 1 and not is_first(k):
                        turn_out(k, (xt_lo_done, 4 * k + 3 if is_last(k) else 4 * k + 5))

            pe.wait_ge(id_in, 16)
            turn_in(0, range(4), None)
            for e in range(2):
                pe.wait_ge(gu_lo_done, e + 1)
                gate_up_of(e, e, 4)
            batches(pe, body)
            if post:
                turn_out(B, (xo_lo_done, 4 * B - 5))


STEPS = 2 * NT


def chunks(s):
    h, i = divmod(s, NT)
    first = 12 * h + (i if i < 4 else 4 + 2 * (i - 4))
    return [(first + c, c, min(CH, P * (i + 1) - CH * c)) for c in range(i // 4 + 1)]


NCHUNK = sum(len(chunks(s)) for s in range(STEPS))
QK_ORDER = [("q", 0), ("q", 1), ("k", 0), ("k", 1), ("q", 2), ("q", 3), ("k", 2), ("k", 3)]
QKV_ORDER = QK_ORDER + [("v", 0), ("v", 1), ("v", 2), ("v", 3)]
QKV_FILLS = dict(zip((0, 2, 3, 4, 6, 7, 8, 10, 11, 12, 14, 15), QKV_ORDER))
OUT_FILLS = {1: 0, 2: 1, 5: 2, 6: 3, 9: 4, 10: 5, 12: 6, 14: 7}
FILLS = []
for _s in range(STEPS):
    if _s in QKV_FILLS:
        FILLS.append(QKV_FILLS[_s])
    if _s in OUT_FILLS:
        FILLS.append(("o", OUT_FILLS[_s]))
WEIGHTS = [(2, "v"), (7, "o"), (9, "q"), (12, "k")]
W_INDEX = {w: n for n, (_, w) in enumerate(WEIGHTS)}
W_FIRST = ["q", "k", "v", "q", "k"]
W_BEFORE = len(W_FIRST)
QK_SPLITS = [(0, 0, 1, 0, 0), (2, 0, 1, 1, 0), (3, 0, 1, 0, 1), (6, 0, 1, 1, 1),
             (8, 1, 0, 0, 0), (10, 1, 0, 1, 0), (15, 1, 0, 0, 1), (15, 1, 0, 1, 1)]
QK_BEFORE = 4
LATE_PRODUCTS = (15,)
RDEN_BEFORE = 1


def bank(kind, idx, m):
    if isinstance(m, int) and m == 0:
        return idx % 2
    return FILLS.index((kind, idx)) % 2


def attention_stage(nc, src, dst, xnt, wq, wk, wv, wo, rope, mask, ident):
    with ExitStack() as ctx:
        def sb(name, shape, dt=F32):
            return ctx.enter_context(nc.sbuf_tensor(name, shape, dt))

        def ps(name, shape):
            return ctx.enter_context(nc.psum_tensor(name, shape, F32))

        def signal(name):
            return ctx.enter_context(nc.semaphore(name))

        raw = {w: sb(f"raw_{w}", [P, KT, 2 * HD]) for w in "qkvo"}
        w_hi = {w: sb(f"w_hi_{w}", [P, KT, 2 * HD], F32R) for w in "qkvo"}
        w_lo = {w: sb(f"w_lo_{w}", [P, KT, 2 * HD], F32R) for w in "qkvo"}
        xt_hi = sb("xt_hi", [P, KT, S], F32R)
        xt_lo = sb("xt_lo", [P, KT, S], F32R)
        x = sb("x", [P, NT, D])
        cs = sb("cs", [P, 4, 2, 256])
        msk = sb("msk", [P, P])
        idn = sb("idn", [P, P])
        prod_a = sb("prod_a", [P, 2, 2, 256])
        prod_b = sb("prod_b", [P, 2, 2, 256])
        rot2 = sb("rot2", [P, 2, CH])
        qk_raw = sb("qk_raw", [P, 2, 2, S])
        qk_hi = sb("qk_hi", [P, 2, 2, S], F32R)
        qk_lo = sb("qk_lo", [P, 2, 2, S], F32R)
        v_raw = sb("v_raw", [P, NT, 2 * HD])
        v_hi = sb("v_hi", [P, NT, 2 * HD], F32R)
        v_lo = sb("v_lo", [P, NT, 2 * HD], F32R)
        probs = sb("probs", [P, 2, S])
        pt_hi = [sb(f"pt_hi{c}", [P, 4 * (c + 1), CH], F32R) for c in range(2)]
        pt_lo = [sb(f"pt_lo{c}", [P, 4 * (c + 1), CH], F32R) for c in range(2)]
        ctx_hi = sb("ctx_hi", [P, CH], F32R)
        ctx_lo = sb("ctx_lo", [P, CH], F32R)
        part_max = sb("part_max", [P, 2, 4])
        neg_max = sb("neg_max", [P, 4])
        den = sb("den", [P, 2, NT, 2])
        den_sum = sb("den_sum", [P, 2, NT])
        rden = sb("rden", [P, 2, NT])
        ps_s = ps("ps_s", [P, 3, CH])
        ps_t = ps("ps_t", [P, 2, CH])
        ps_c = ps("ps_c", [P, CH])
        ps_f = ps("ps_f", [P, 2, CH])

        const_in = signal("const_in")
        raw_in = {w: signal(f"raw_in_{w}") for w in "qkvo"}
        q_scaled = signal("q_scaled")
        w_hi_done = signal("w_hi_done")
        w_lo_done = signal("w_lo_done")
        xt_in = [signal(f"xt_in{half}") for half in range(2)]
        x_in = [signal(f"x_in{c}") for c in range(2)]
        x_out = [signal(f"x_out{c}") for c in range(2)]
        zeroed = signal("zeroed")
        qk_filled = signal("qk_filled")
        v_filled = signal("v_filled")
        out_filled = signal("out_filled")
        prod_done = signal("prod_done")
        rot_done = signal("rot_done")
        parted = signal("parted")
        shifted = [signal(f"shifted{g}") for g in range(4)]
        qk_hi_done = signal("qk_hi_done")
        qk_lo_done = signal("qk_lo_done")
        v_raw_done = signal("v_raw_done")
        v_hi_done = signal("v_hi_done")
        v_lo_done = signal("v_lo_done")
        scored = signal("scored")
        part_done = signal("part_done")
        max_done = signal("max_done")
        exp_done = signal("exp_done")
        p_turned = signal("p_turned")
        pt_hi_done = signal("pt_hi_done")
        pt_lo_done = signal("pt_lo_done")
        pv_done = signal("pv_done")
        ctx_hi_done = signal("ctx_hi_done")
        ctx_lo_done = signal("ctx_lo_done")
        den_summed = signal("den_summed")
        rden_done = signal("rden_done")
        out_added = signal("out_added")
        sp_own = signal("sp_own")
        dve_own = signal("dve_own")

        def batches(eng, body):
            with eng.Fori(0, B) as b:
                body(b * PAIRS, b, "first")
                with eng.Fori(1, PAIRS - 1) as p:
                    body(b * PAIRS + p, b, "middle")
                body(b * PAIRS + PAIRS - 1, b, "last")

        def weight_view(t, w):
            return t[:, :, :].rearrange("p k (two f) -> p k two f", two=2) if w in "qk" else t[:, :, :]

        def raw_view(w):
            return raw[w][:, :, :].rearrange("p k (f two) -> p k two f", two=2) if w in "qk" else raw[w][:, :, :]

        block = ctx.enter_context(nc.Block())

        @block.sync
        def _(sp):
            w_dram = {"q": wq, "k": wk, "v": wv}

            def load_raw(w, pair):
                if w == "o":
                    view = wo[bass.ds(pair * 2 * HD, 2 * HD), :].rearrange("(h p) d -> p h d", p=P)
                else:
                    view = w_dram[w][:, bass.ds(pair * 2 * HD, 2 * HD)].rearrange("(k p) n -> p k n", p=P)
                sp.dma_start(raw[w][:, :, :], view).then_inc(raw_in[w], 16)

            def load_xt(batch, half):
                toks = slice(CH * half, CH * half + CH)
                sp.dma_start(f(xt_hi[:, :, toks]), xnt[batch, 0][:, :, toks]).then_inc(xt_in[half], 16)
                sp.dma_start(f(xt_lo[:, :, toks]), xnt[batch, 1][:, :, toks]).then_inc(xt_in[half], 16)

            def shift(m, g):
                sp.wait_ge(rot_done, 8 * m + 2 * g + 2)
                sp.sem_inc(sp_own, 1)
                kind, cols = g % 2, slice(CH * (g // 2), CH * (g // 2) + CH)
                sp.dma_start(qk_raw[HALF:P, kind, 1, cols], qk_raw[HALF:P, kind, 0, cols]).then_inc(parted, 16)
                sp.dma_start(qk_raw[0:HALF, kind, 1, cols], rot2[HALF:P, g % 2]).then_inc(shifted[g], 16)
                sp.wait_ge(parted, 16 * (4 * m + g + 1))
                sp.sem_inc(sp_own, 1)
                sp.dma_start(qk_raw[HALF:P, kind, 0, cols], rot2[0:HALF, g % 2]).then_inc(shifted[g], 16)

            def rows(t, b, c):
                return t[b].rearrange("(t p) d -> p t d", p=P)[:, 4 * c:4 * c + 4]

            def turn_over_x(n, b, c, store):
                sp.wait_ge(out_added, 8 * n + 2 * c + 2 + OUT_ADDED_CREDIT)
                sp.sem_inc(sp_own, 1)
                if store:
                    sp.dma_start(rows(dst, b - 1, c), x[:, 4 * c:4 * c + 4]).then_inc(x_out[c], 16)
                    sp.wait_ge(x_out[c], 16 * b)
                    sp.sem_inc(sp_own, 1)
                sp.dma_start(x[:, 4 * c:4 * c + 4], rows(src, b, c)).then_inc(x_in[c], 16)

            def body(n, b, p, kind, store=True):
                def next_raw(w, at):
                    sp.wait_ge(w_lo_done, W_BEFORE + 4 * n + W_INDEX[w] + 1)
                    sp.sem_inc(sp_own, 1)
                    load_raw(w, (p + at) % PAIRS)

                if kind == "last":
                    for half in range(2):
                        sp.wait_ge(v_filled, 4 * n + 2 * half + 2)
                        sp.sem_inc(sp_own, 1)
                        load_xt((b + 1) % B, half)
                for s in range(STEPS):
                    if s in QKV_FILLS and QKV_FILLS[s][0] != "v" and QK_ORDER.index(QKV_FILLS[s]) % 2:
                        shift(n + 1, QK_ORDER.index(QKV_FILLS[s]) // 2)
                    for step, w in WEIGHTS:
                        if step == s:
                            next_raw(w, {"v": 2, "o": 1, "q": 3, "k": 3}[w])
                    if kind == "first" and OUT_FILLS.get(s) in (1, 3):
                        turn_over_x(n, b, OUT_FILLS[s] // 2, store)

            def batch(b, store):
                body(b * PAIRS, b, 0, "first", store)
                with sp.Fori(1, PAIRS - 1) as p:
                    body(b * PAIRS + p, b, p, "middle")
                body(b * PAIRS + PAIRS - 1, b, PAIRS - 1, "last")

            for half in range(2):
                load_xt(0, half)
            for w in "qkv":
                load_raw(w, 0)
            sp.dma_start(cs[:, :, :, :], rope).then_inc(const_in, 16)
            sp.dma_start(msk[:, :], mask).then_inc(const_in, 16)
            sp.dma_start(idn[:, :], ident).then_inc(const_in, 16)
            load_raw("o", 0)
            for n, w in enumerate(W_FIRST[:3]):
                sp.wait_ge(w_lo_done, n + 1)
                load_raw(w, 1)
            for g in range(4):
                shift(0, g)
            for n, w in enumerate(W_FIRST[3:]):
                sp.wait_ge(w_lo_done, 3 + n + 1)
                load_raw(w, 2)
            batch(0, False)
            with sp.Fori(1, B) as b:
                batch(b, True)
            for c in range(2):
                sp.wait_ge(out_added, 8 * NPAIR + 2 * c + 2 + OUT_ADDED_CREDIT)
                sp.dma_start(rows(dst, B - 1, c), x[:, 4 * c:4 * c + 4]).then_inc(x_out[c], 16)
            for c in range(2):
                sp.wait_ge(x_out[c], 16 * B)
            for w in "qkvo":
                sp.wait_ge(raw_in[w], 16 * (NPAIR + {"q": 3, "k": 3, "v": 2, "o": 1}[w]))

        @block.gpsimd
        def _(pool):
            def weight_lo(w, count, used, n_used):
                pool.wait_ge(w_hi_done, count)
                if used is not None:
                    pool.wait_ge(used, n_used)
                pool.tensor_tensor(weight_view(w_lo[w], w), raw_view(w), weight_view(f(w_hi[w][:, :, :]), w),
                                   ALU.subtract).then_inc(w_lo_done, 1)

            def rotate(m, idx):
                g = idx // 2
                kind, t = "qk".index(QK_ORDER[idx][0]), QK_ORDER[idx][1]
                cols = slice(256 * t, 256 * t + 256)
                pool.wait_ge(prod_done, 8 * m + idx + 1)
                if idx % 2 == 0 and not isinstance(m, int):
                    pool.wait_ge(qk_lo_done, QK_BEFORE + 8 * (m - 1) + g + 1)
                if idx % 2 == 0:
                    before = 32 * (m + 1) if g >= 2 else 32 * m
                    if not (isinstance(before, int) and before == 0):
                        pool.wait_ge(shifted[(g + 2) % 4], before)
                pool.tensor_tensor(qk_raw[:, kind, 0, cols], prod_a[:, idx % 2, 0], prod_a[:, idx % 2, 1], ALU.subtract)
                pool.tensor_tensor(rot2[:, g % 2, 256 * (t % 2):256 * (t % 2) + 256], prod_b[:, idx % 2, 0],
                                   prod_b[:, idx % 2, 1], ALU.add).then_inc(rot_done, 1)

            def qk_low(count, h, kind, half):
                toks = slice(CH * half, CH * half + CH)
                pool.wait_ge(qk_hi_done, count)
                pool.tensor_tensor(qk_lo[:, kind, h, toks], qk_raw[:, kind, h, toks], f(qk_hi[:, kind, h, toks]),
                                   ALU.subtract).then_inc(qk_lo_done, 1)

            def v_low(m, h):
                pool.wait_ge(v_hi_done, 2 * m + h + 1)
                cols = slice(HD * h, HD * h + HD)
                pool.tensor_tensor(v_lo[:, :, cols], v_raw[:, :, cols], f(v_hi[:, :, cols]),
                                   ALU.subtract).then_inc(v_lo_done, 1)

            def body(n, b, kind_of_body):
                for s in range(STEPS):
                    for j, (step, _, h, kind, half) in enumerate(QK_SPLITS):
                        if step == s:
                            qk_low(QK_BEFORE + 8 * n + j + 1, h, kind, half)
                    if s in QKV_FILLS and QKV_FILLS[s][0] != "v":
                        rotate(n + 1, QK_ORDER.index(QKV_FILLS[s]))
                    if s == 2:
                        v_low(n, 0)
                    if s == 5:
                        v_low(n, 1)
                    for idx, (step, w) in enumerate(WEIGHTS):
                        if step == s:
                            used, count = {"v": (v_filled, 4 * n + 4), "o": (out_filled, 8 * n + 4 + OUT_FILLED_CREDIT),
                                           "q": (qk_filled, 8 * n + 14), "k": (qk_filled, 8 * n + 16)}[w]
                            weight_lo(w, W_BEFORE + 4 * n + idx + 1, used, count)

            pool.memset(f(pt_hi[1][:, :, :]), 0.0).then_inc(zeroed, 1)
            pool.memset(f(v_lo[:, :, HD:]), 0.0).then_inc(zeroed, 1)
            for n, w in enumerate(W_FIRST):
                if n == 3:
                    for idx in range(8):
                        rotate(0, idx)
                    for j in range(4):
                        qk_low(j + 1, 0, j % 2, j // 2)
                weight_lo(w, n + 1, qk_filled if n >= 3 else None, 8)
            batches(pool, body)

        @block.scalar
        def _(act):
            def v_copy(m, idx):
                act.wait_ge(v_filled, 4 * m + idx + 1)
                act.activation(v_raw[:, 2 * idx:2 * idx + 2].rearrange("p t d -> p (t d)"), ps_f[:, bank("v", idx, m)],
                               ACT.Copy).then_inc(v_raw_done, 1)

            def qk_high(m, h, kind, half, n_scored):
                g = 2 * half + kind
                toks = slice(CH * half, CH * half + CH)
                act.wait_ge(rot_done, 8 * m + 2 * g + 2)
                act.wait_ge(shifted[g], 32 * (m + 1))
                if n_scored is not None:
                    act.wait_ge(scored, n_scored)
                act.activation(qk_hi[:, kind, h, toks], qk_raw[:, kind, h, toks], ACT.Copy).then_inc(qk_hi_done, 1)

            def v_high(m, h, sig, n):
                act.wait_ge(v_raw_done, 4 * m + 4)
                act.wait_ge(sig, n)
                cols = slice(HD * h, HD * h + HD)
                act.activation(v_hi[:, :, cols], v_raw[:, :, cols], ACT.Copy).then_inc(v_hi_done, 1)

            def exps(n, s, slot_used=True):
                act.wait_ge(max_done, STEPS * n + s + 1)
                if slot_used:
                    before = chunks(s - 2)[-1][0] if s >= 2 else chunks(s - 2 + STEPS)[-1][0] - NCHUNK
                    act.wait_ge(p_turned, NCHUNK * n + before + 1 + P_TURNED_CREDIT)
                h, i = divmod(s, NT)
                for ci, c, k in chunks(s):
                    act.activation(probs[:, s % 2, CH * c:CH * c + k], ps_s[:, ci % 3, 0:k], ACT.Exp,
                                   bias=neg_max[:, s % 4:s % 4 + 1],
                                   accum_out=den[:, h, i, c:c + 1]).then_inc(exp_done, 1)

            def pt_high(n, s, ci, c, k):
                i = s % NT
                act.wait_ge(p_turned, NCHUNK * n + ci + 1 + P_TURNED_CREDIT)
                act.activation(pt_hi[i // 4][:, 4 * c:4 * c + k // P, P * (i % 4):P * (i % 4) + P],
                               ps_t[:, ci % 2, 0:k].rearrange("p (j q) -> p j q", q=P), ACT.Copy).then_inc(pt_hi_done, 1)

            def ctx_high(n, k):
                act.wait_ge(pv_done, 4 * n + k + 1)
                act.wait_ge(out_filled, 8 * n + 2 * k + 2 + OUT_FILLED_CREDIT)
                act.activation(ctx_hi[:, :], ps_c[:, :], ACT.Copy).then_inc(ctx_hi_done, 1)

            def body(n, b, kind_of_body):
                for s in range(STEPS):
                    if s in QKV_FILLS and QKV_FILLS[s][0] == "v":
                        if QKV_FILLS[s][1] == 0:
                            act.wait_ge(v_lo_done, 2 * n + 2)
                        v_copy(n + 1, QKV_FILLS[s][1])
                    m, nxt = (n, s + 1) if s + 1 < STEPS else (n + 1, 0)
                    if len(chunks(nxt)) == 1:
                        exps(m, nxt)
                    for ci, c, k in chunks(s):
                        pt_high(n, s, ci, c, k)
                    if s % 4 == 3:
                        ctx_high(n, s // 4)
                    if len(chunks(nxt)) > 1:
                        exps(m, nxt)
                    for step, w in WEIGHTS:
                        if step == s:
                            if w == "q":
                                act.wait_ge(q_scaled, n + 3)
                            else:
                                act.wait_ge(raw_in[w], 16 * n + {"v": 32, "o": 16, "k": 48}[w])
                            used, count = {"v": (v_filled, 4 * n + 4), "o": (out_filled, 8 * n + 4 + OUT_FILLED_CREDIT),
                                           "q": (qk_filled, 8 * n + 14), "k": (qk_filled, 8 * n + 16)}[w]
                            act.wait_ge(used, count)
                            act.activation(weight_view(w_hi[w], w), raw_view(w), ACT.Copy).then_inc(w_hi_done, 1)
                    for step, ahead, h, kind, half in QK_SPLITS:
                        if step == s:
                            qk_high(n + ahead, h, kind, half, NCHUNK * n + (NCHUNK // 2 if ahead else 1))
                    if s == 2:
                        v_high(n, 0, p_turned, NCHUNK * n + 1 + P_TURNED_CREDIT)
                    if s == 5:
                        v_high(n, 1, pv_done, 4 * n + 1)

            act.sem_inc(exp_done, EXP_DONE_CREDIT)
            for n, w in enumerate(W_FIRST):
                if n == 3:
                    for idx in range(4):
                        v_copy(0, idx)
                    for j in range(4):
                        qk_high(0, 0, j % 2, j // 2, None)
                    act.wait_ge(qk_filled, 8)
                if w == "q":
                    act.wait_ge(q_scaled, 1 + n // 3)
                else:
                    act.wait_ge(raw_in[w], 16 + 16 * (n // 3))
                act.activation(weight_view(w_hi[w], w), raw_view(w), ACT.Copy).then_inc(w_hi_done, 1)
            exps(0, 0, False)
            batches(act, body)
            ctx_high(NPAIR, 0)

        @block.vector
        def _(dve):
            def scale_q(m):
                dve.wait_ge(raw_in["q"], 16 * (m + 1))
                dve.tensor_scalar(raw["q"][:, :, :], raw["q"][:, :, :], float(1.0 / np.sqrt(HD)), None,
                                  ALU.mult).then_inc(q_scaled, 1)

            def products(m, idx):
                kind, t = QK_ORDER[idx]
                pair = ps_f[:, bank(kind, t, m)].rearrange("p (a n) -> p a n", a=2)
                dve.wait_ge(qk_filled, 8 * m + idx + 1)
                before = 8 * m + idx - 1
                if not (isinstance(before, int) and before <= 0):
                    dve.wait_ge(rot_done, before)
                dve.tensor_tensor(prod_a[:, idx % 2], pair, cs[:, t], ALU.mult)
                dve.tensor_tensor(prod_b[:, idx % 2], pair, cs[:, t, ::-1], ALU.mult).then_inc(prod_done, 1)

            parts = [0]
            for s in range(STEPS):
                i = s % NT
                parts.append(parts[-1] + (1 if i == 0 else 2 if i <= 4 else 3))

            def part_maxima(n, s, which):
                i = s % NT
                ci, c, k = chunks(s)[which]
                at = which
                dve.wait_ge(scored, NCHUNK * n + ci + 1)
                if c == i // 4:
                    dve.sem_inc(dve_own, 1)
                    own = ps_s[:, ci % 3, k - P:k]
                    dve.tensor_tensor_reduce(own, own, msk[:, :], 1.0, -3e38, ALU.add, ALU.max,
                                             part_max[:, s % 2, at:at + 1]).then_inc(part_done, 1)
                    at += 1
                    k -= P
                if k:
                    dve.tensor_reduce(part_max[:, s % 2, at:at + 1], ps_s[:, ci % 3, 0:k], AX.X, ALU.max)\
                       .then_inc(part_done, 1)
                    at += 1
                if c == i // 4:
                    dve.wait_ge(part_done, (parts[STEPS] * n if not isinstance(n, int) else 0) + parts[s] + at)
                    dve.tensor_reduce(neg_max[:, s % 4:s % 4 + 1], part_max[:, s % 2, 0:at], AX.X, ALU.max,
                                      negate=True).then_inc(max_done, 1)

            def pt_low(n, s, ci, c, k):
                i = s % NT
                at = (slice(4 * c, 4 * c + k // P), slice(P * (i % 4), P * (i % 4) + P))
                dve.wait_ge(pt_hi_done, NCHUNK * n + ci + 1)
                dve.tensor_tensor(pt_lo[i // 4][:, at[0], at[1]], ps_t[:, ci % 2, 0:k].rearrange("p (j q) -> p j q", q=P),
                                  f(pt_hi[i // 4][:, at[0], at[1]]), ALU.subtract).then_inc(pt_lo_done, 1)

            def ctx_low(n, k):
                dve.wait_ge(ctx_hi_done, 4 * n + k + 1)
                dve.tensor_tensor(ctx_lo[:, :], ps_c[:, :], f(ctx_hi[:, :]), ALU.subtract).then_inc(ctx_lo_done, 1)

            def reciprocal(n, r):
                h, c = divmod(r, 2)
                blocks = slice(4 * c, 4 * c + 4)
                dve.wait_ge(exp_done, NCHUNK * n + chunks(NT * h + 4 * c + 3)[-1][0] + 1 + EXP_DONE_CREDIT)
                if c:
                    dve.tensor_tensor(den_sum[:, h, blocks], den[:, h, blocks, 0], den[:, h, blocks, 1],
                                      ALU.add).then_inc(den_summed, 1)
                    dve.wait_ge(den_summed, 2 * n + h + 1)
                    dve.reciprocal(rden[:, h, blocks], den_sum[:, h, blocks]).then_inc(rden_done, 1)
                else:
                    dve.reciprocal(rden[:, h, blocks], den[:, h, blocks, 0]).then_inc(rden_done, 1)

            def add_out(n, w, kind):
                h = 1 if w < 4 else 0
                dve.wait_ge(out_filled, 8 * n + w + 1 + OUT_FILLED_CREDIT)
                for u in range(2):
                    t = 4 * (w // 2 % 2) + 2 * (w % 2) + u
                    last = dve.scalar_tensor_tensor(out=x[:, t], in0=ps_f[:, bank("o", w, n), D * u:D * u + D],
                                                    scalar=rden[:, h, t:t + 1], in1=x[:, t], op0=ALU.mult, op1=ALU.add)
                last.then_inc(out_added, 1)

            def body(n, b, kind_of_body):
                for s in range(STEPS):
                    m, nxt = (n, s + 1) if s + 1 < STEPS else (n + 1, 0)
                    if s == 7:
                        scale_q(n + 2)
                    part_maxima(m, nxt, 0)
                    work = chunks(s)
                    if s in LATE_PRODUCTS:
                        pt_low(n, s, *work[0])
                    if s in QKV_FILLS and QKV_FILLS[s][0] != "v":
                        products(n + 1, QK_ORDER.index(QKV_FILLS[s]))
                    if s not in LATE_PRODUCTS:
                        pt_low(n, s, *work[0])
                    if len(chunks(nxt)) > 1:
                        part_maxima(m, nxt, 1)
                    if len(work) > 1:
                        pt_low(n, s, *work[1])
                    if s in OUT_FILLS:
                        w = OUT_FILLS[s]
                        if w % 2 == 0:
                            dve.wait_ge(rden_done, 4 * n + w // 2 - 1 + RDEN_BEFORE)
                        if kind_of_body == "first" and w in (4, 6):
                            dve.wait_ge(x_in[w // 2 - 2], 16 * b + 16)
                        add_out(n, w, kind_of_body)
                    if s in (4, 8, 12, 15):
                        reciprocal(n, {4: 0, 8: 1, 12: 2, 15: 3}[s])
                    if s % 4 == 3:
                        ctx_low(n, s // 4)

            for t in (pt_lo[1][:, :, :], v_hi[:, :, HD:], ctx_hi[:, :], ctx_lo[:, :], w_hi["o"][:, :, :], w_lo["o"][:, :, :]):
                dve.memset(f(t), 0.0).then_inc(zeroed, 1)
            dve.memset(x[:, :, :], 0.0).then_inc(zeroed, 1)
            dve.memset(rden[:, :, :], 0.0).then_inc(rden_done, RDEN_BEFORE)
            dve.sem_inc(pt_lo_done, PT_LO_DONE_CREDIT)
            dve.sem_inc(ctx_lo_done, CTX_LO_DONE_CREDIT)
            dve.sem_inc(out_added, OUT_ADDED_CREDIT)
            scale_q(0)
            dve.wait_ge(const_in, 48)
            for idx in range(8):
                products(0, idx)
            scale_q(1)
            part_maxima(0, 0, 0)
            batches(dve, body)
            add_out(NPAIR, 0, None)
            add_out(NPAIR, 1, None)
            ctx_low(NPAIR, 0)
            add_out(NPAIR, 2, None)
            add_out(NPAIR, 3, None)

        @block.tensor
        def _(pe):
            def bank_free(n, kind, idx):
                at = FILLS.index((kind, idx)) - 2
                before, j = FILLS[at]
                back = 1 if at < 0 else 0
                if before == "o":
                    pe.wait_ge(out_added, 8 * (n - back) + j + 1 + OUT_ADDED_CREDIT)
                elif before == "v":
                    pe.wait_ge(v_raw_done, 4 * (n + 1 - back) + j + 1)
                else:
                    pe.wait_ge(prod_done, 8 * (n + 1 - back) + QK_ORDER.index((before, j)) + 1)

            def fill(m, kind, idx):
                out = ps_f[:, bank(kind, idx, m)]
                if kind == "v":
                    for u in range(2):
                        t = 2 * idx + u
                        n = 0
                        for kt in range(KT):
                            cols = slice(P * t, P * t + P)
                            for a, w in passes(xt_hi[:, kt, cols], xt_lo[:, kt, cols], w_hi["v"][:, kt], w_lo["v"][:, kt]):
                                last = pe.matmul(out[:, 256 * u:256 * u + 256], a, w, start=n == 0, stop=n == 5)
                                n += 1
                    last.then_inc(v_filled, 1)
                    return
                for two in range(2):
                    n = 0
                    for kt in range(KT):
                        cols, toks = slice(P * two, P * two + P), slice(256 * idx, 256 * idx + 256)
                        for w, a in passes(w_hi[kind][:, kt, cols], w_lo[kind][:, kt, cols], xt_hi[:, kt, toks], xt_lo[:, kt, toks]):
                            last = pe.matmul(out[:, 256 * two:256 * two + 256], w, a, start=n == 0, stop=n == 5)
                            n += 1
                last.then_inc(qk_filled, 1)

            def fill_out(w):
                h = 1 if w < 4 else 0
                for u in range(2):
                    cols = slice(P * (2 * (w % 2) + u), P * (2 * (w % 2) + u) + P)
                    n = 0
                    for a, ww in passes(ctx_hi[:, cols], ctx_lo[:, cols], w_hi["o"][:, h], w_lo["o"][:, h]):
                        last = pe.matmul(ps_f[:, bank("o", w, None), D * u:D * u + D], a, ww, start=n == 0, stop=n == 2)
                        n += 1
                last.then_inc(out_filled, 1)

            def scores(n, s, which):
                h, i = divmod(s, NT)
                ci, c, k = chunks(s)[which]
                pe.wait_ge(exp_done, NCHUNK * n + ci - 2 + EXP_DONE_CREDIT)
                j = 0
                for q, kk in passes(qk_hi[:, 0, h, P * i:P * i + P], qk_lo[:, 0, h, P * i:P * i + P],
                                    qk_hi[:, 1, h, CH * c:CH * c + k], qk_lo[:, 1, h, CH * c:CH * c + k]):
                    last = pe.matmul(ps_s[:, ci % 3, 0:k], q, kk, start=j == 0, stop=j == 2)
                    j += 1
                last.then_inc(scored, 1)

            def turn(n, s, which):
                ci, c, k = chunks(s)[which]
                pe.wait_ge(exp_done, NCHUNK * n + ci + 1 + EXP_DONE_CREDIT)
                pe.wait_ge(pt_lo_done, NCHUNK * n + ci - 1 + PT_LO_DONE_CREDIT)
                for j in range(k // P):
                    last = pe.transpose(ps_t[:, ci % 2, P * j:P * j + P], probs[:, s % 2, CH * c + P * j:CH * c + P * j + P], idn[:, :])
                last.then_inc(p_turned, 1)

            def context(h, c, blocks):
                final = 4 * c + 3
                for j in blocks:
                    first = max(0, P * (j - 4 * c))
                    v = (v_hi[:, j, HD * h:HD * h + HD], v_lo[:, j, HD * h:HD * h + HD])
                    p_ = (pt_hi[c][:, j, first:], pt_lo[c][:, j, first:])
                    for m, (a, b) in enumerate(passes(*v, *p_)):
                        last = pe.matmul(ps_c[:, first:], a, b, start=j == 0 and m == 0, stop=j == final and m == 2)
                if final in blocks:
                    last.then_inc(pv_done, 1)

            def add_context(n, h, i):
                if i == 0:
                    pe.wait_ge(ctx_lo_done, 4 * n + 2 * h + CTX_LO_DONE_CREDIT)
                    pe.wait_ge(pt_lo_done, NCHUNK * n + 12 * h + PT_LO_DONE_CREDIT)
                if i == 4:
                    pe.wait_ge(ctx_lo_done, 4 * n + 2 * h + 1 + CTX_LO_DONE_CREDIT)
                    pe.wait_ge(pt_lo_done, NCHUNK * n + 12 * h + 4 + PT_LO_DONE_CREDIT)
                    pe.wait_ge(v_lo_done, 2 * n + h + 1)
                if i < 4:
                    context(1 - h, 1, (2 * i, 2 * i + 1))
                else:
                    context(h, 0, (i - 4,))

            def body(n, b, kind_of_body):
                for s in range(STEPS):
                    h, i = divmod(s, NT)
                    m, nxt = (n, s + 1) if s + 1 < STEPS else (n + 1, 0)
                    if s == 3:
                        pe.wait_ge(qk_lo_done, QK_BEFORE + 8 * n)
                    if s in (7, 11):
                        pe.wait_ge(qk_lo_done, QK_BEFORE + 8 * n + (2 if s == 7 else 4))
                    if s == STEPS - 1:
                        pe.wait_ge(qk_lo_done, QK_BEFORE + 8 * n + 6)
                    scores(m, nxt, 0)
                    if s in QKV_FILLS:
                        kind, idx = QKV_FILLS[s]
                        if kind == "q" and idx in (0, 2) and kind_of_body == "last":
                            pe.wait_ge(xt_in[idx // 2], 32 * b + 64)
                        if idx == 0:
                            pe.wait_ge(w_lo_done, {"q": 4 * n + 4, "k": 4 * n + 5, "v": W_BEFORE + 4 * n + 1}[kind])
                        bank_free(n, kind, idx)
                        fill(n + 1, kind, idx)
                    if i % 4:
                        add_context(n, h, i)
                    turn(n, s, 0)
                    if len(chunks(nxt)) > 1:
                        scores(m, nxt, 1)
                    if s in OUT_FILLS:
                        w = OUT_FILLS[s]
                        if w % 2 == 0:
                            pe.wait_ge(ctx_lo_done, 4 * n + w // 2 + CTX_LO_DONE_CREDIT)
                        if w == 4:
                            pe.wait_ge(w_lo_done, W_BEFORE + 4 * n + W_INDEX["o"] + 1)
                        bank_free(n, "o", w)
                        fill_out(w)
                    if len(chunks(s)) > 1:
                        turn(n, s, 1)
                    if i % 4 == 0:
                        add_context(n, h, i)

            pe.sem_inc(out_filled, OUT_FILLED_CREDIT)
            pe.sem_inc(p_turned, P_TURNED_CREDIT)
            for half in range(2):
                pe.wait_ge(xt_in[half], 32)
            order = QKV_ORDER
            for at, (kind, idx) in enumerate(order):
                if idx == 0:
                    pe.wait_ge(w_lo_done, "qkv".index(kind) + 1)
                if at >= 2:
                    before, j = order[at - 2]
                    if before == "v":
                        pe.wait_ge(v_raw_done, j + 1)
                    else:
                        pe.wait_ge(prod_done, QK_ORDER.index((before, j)) + 1)
                fill(0, kind, idx)
            pe.wait_ge(const_in, 48)
            pe.wait_ge(qk_lo_done, 2)
            scores(0, 0, 0)
            pe.wait_ge(v_raw_done, 4)
            pe.wait_ge(zeroed, 9)
            batches(pe, body)
            n = NPAIR
            for w in range(2):
                pe.wait_ge(ctx_lo_done, 4 * n + CTX_LO_DONE_CREDIT)
                bank_free(n, "o", w)
                fill_out(w)
            pe.wait_ge(pt_lo_done, NCHUNK * n + PT_LO_DONE_CREDIT)
            context(1, 1, range(8))
            for w in range(2, 4):
                pe.wait_ge(ctx_lo_done, 4 * n + 1 + CTX_LO_DONE_CREDIT)
                pe.wait_ge(out_added, 8 * n + w + OUT_ADDED_CREDIT)
                fill_out(w)


def constants():
    freqs = 1.0 / 10000.0 ** (np.arange(0, HD, 2, dtype=np.float32) / HD)
    ang = np.outer(np.arange(S, dtype=np.float32), freqs)
    table = np.stack([np.cos(ang), np.sin(ang)]).transpose(2, 0, 1)
    table = table.reshape(HALF, 2, 4, 256).transpose(0, 2, 1, 3)
    return {
        "rope": np.ascontiguousarray(np.concatenate([table, table]), dtype=np.float32),
        "mask": np.triu(np.full((P, P), NEG, np.float32), 1),
        "ident": np.eye(P, dtype=np.float32),
    }


_INS = ['L0_attn_x', 'L0_attn_Wq', 'L0_attn_Wk', 'L0_attn_Wv', 'L0_attn_Wo', 'L0_ffn_gate_up_proj', 'L0_ffn_down_proj']


def macaron(nc, x, wq, wk, wv, wo, gate_up, down, rope, mask, ident, out):
    x1 = nc.dram_tensor("x1", [B, S, D], F32).ap()
    x2 = nc.dram_tensor("x2", [B, S, D], F32).ap()
    xnt = nc.dram_tensor("xnt", [B, 2, P, KT * S], F32).ap().rearrange("b h p (k t) -> b h p k t", k=KT)
    ffn_stage(nc, "ffn1_", x, x1, gate_up, down, ident, xnt)
    attention_stage(nc, x1, x2, xnt, wq, wk, wv, wo, rope, mask, ident)
    ffn_stage(nc, "ffn2_", x2, out, gate_up, down, ident, None)


def kernel(**inputs):
    import numpy as _np
    import concourse.bacc as _bacc
    from concourse import mybir as _mybir
    from concourse.bass_utils import run_bass_kernel_spmd as _run

    nc = _bacc.Bacc("TRN2", target_bir_lowering=False, num_devices=1)
    arrays, args = {}, []
    for name, value in [(name, inputs[name]) for name in _INS] + list(constants().items()):
        a = _np.ascontiguousarray(value)
        arrays[f"in_{name}_dram"] = a
        args.append(nc.dram_tensor(f"in_{name}_dram", a.shape, _mybir.dt.from_np(a.dtype), kind="ExternalInput").ap())
    args.append(nc.dram_tensor("out_0_dram", (B, S, D), F32, kind="ExternalOutput").ap())
    macaron(nc, *args)
    r = _run(nc, [arrays], core_ids=[0])
    return r.results[0]["out_0_dram"]
```

```python
from contextlib import ExitStack

import concourse.bass as bass
import numpy as np
from concourse import mybir

ALU = mybir.AluOpType
ACT = mybir.ActivationFunctionType
AX = mybir.AxisListType
F32 = mybir.dt.float32
F32R = mybir.dt.float32r

P = 128
B, S, D = 4, 1024, 256
H, HD = 16, 128
E, I = 4, 256
EPS = 1e-5
NEG = -1e30
KT = D // P
CH = 512
NCH = S // CH
NT = S // P
PAIRS = H // 2
NPAIR = B * PAIRS
HALF = HD // 2


CTX_LO_DONE_CREDIT = 1
EXP_DONE_CREDIT = 3
INNER_DONE_CREDIT = 2
INNER_LO_CREDIT = 2
OUT_ADDED_CREDIT = 1
OUT_FILLED_CREDIT = 1
P_TURNED_CREDIT = 3
PT_LO_DONE_CREDIT = 2
XNT_STORED_CREDIT = 32
Y_DONE_CREDIT = 2


def passes(hi_a, lo_a, hi_b, lo_b):
    return (hi_a, hi_b), (hi_a, lo_b), (lo_a, hi_b)


def f(ap):
    return ap.bitcast(F32)


def ffn_stage(nc, tag, src, dst, gate_up, down, ident, xnt):
    post = xnt is not None
    with ExitStack() as ctx:
        def sb(name, shape, dt=F32):
            return ctx.enter_context(nc.sbuf_tensor(tag + name, shape, dt))

        def ps(name, shape):
            return ctx.enter_context(nc.psum_tensor(tag + name, shape, F32))

        def signal(name):
            return ctx.enter_context(nc.semaphore(tag + name))

        gu_raw = sb("gu_raw", [P, E, KT, 2 * I])
        gu_hi = sb("gu_hi", [P, E, KT, 2 * I], F32R)
        gu_lo = sb("gu_lo", [P, E, KT, 2 * I], F32R)
        dn_raw = sb("dn_raw", [P, E, KT, D])
        dn_hi = sb("dn_hi", [P, E, KT, D], F32R)
        dn_lo = sb("dn_lo", [P, E, KT, D], F32R)
        idn = sb("idn", [P, P])
        x_in = sb("x_in", [P, NCH, E, D])
        xn = sb("xn", [P, NCH, E, D])
        xt_hi = sb("xt_hi", [P, KT, E, NCH, P], F32R)
        xt_lo = sb("xt_lo", [P, KT, E, NCH, P], F32R)
        x_out = sb("x_out", [P, NCH, E, D])
        xn_out = sb("xn_out", [P, NCH, E, D])
        xo_hi = sb("xo_hi", [P, KT, S], F32R)
        xo_lo = sb("xo_lo", [P, KT, S], F32R)
        mhalf = sb("mhalf", [P, E])
        stats = sb("stats", [P, NCH, E, 6])
        mv = sb("mv", [P, NCH, E, 2])
        var = sb("var", [P, NCH, E])
        minus_mean = sb("minus_mean", [P, NCH, E])
        rstd = sb("rstd", [P, NCH, E])
        shift_in = sb("shift_in", [P, NCH, E])
        o_stats = sb("o_stats", [P, 2, NCH, 6])
        o_mv = sb("o_mv", [P, 2, NCH, 2])
        o_var = sb("o_var", [P, 2, NCH])
        o_minus_mean = sb("o_minus_mean", [P, 2, NCH])
        o_rstd = sb("o_rstd", [P, 2, NCH])
        o_shift = sb("o_shift", [P, 2, NCH])
        sig = sb("sig", [P, 2, CH])
        silu_g = sb("silu_g", [P, 2, CH])
        inner = sb("inner", [P, 2, CH])
        in_hi = sb("in_hi", [P, 2, 2, D], F32R)
        in_lo = sb("in_lo", [P, 2, 2, D], F32R)
        ps_t = ps("ps_t", [P, 2, CH])
        ps_g = ps("ps_g", [P, 2, CH])
        ps_u = ps("ps_u", [P, 2, CH])
        ps_y = ps("ps_y", [P, 2, CH])

        w_in = [signal(f"w_in{e}") for e in range(E)]
        id_in = signal("id_in")
        gu_hi_done = signal("gu_hi_done")
        dn_hi_done = signal("dn_hi_done")
        gu_lo_done = signal("gu_lo_done")
        dn_lo_done = signal("dn_lo_done")
        x_loaded = [signal(f"x_loaded{c}") for c in range(NCH)]
        half_set = signal("half_set")
        stats_done = signal("stats_done")
        mv_done = signal("mv_done")
        var_done = signal("var_done")
        rstd_step = signal("rstd_step")
        shift_done = signal("shift_done")
        xn_done = signal("xn_done")
        res_in = [signal(f"res_in{e}") for e in range(E)]
        xt_turned = signal("xt_turned")
        xt_hi_done = signal("xt_hi_done")
        xt_lo_done = signal("xt_lo_done")
        xo_turned = signal("xo_turned")
        xo_hi_done = signal("xo_hi_done")
        xo_lo_done = signal("xo_lo_done")
        gu_done = signal("gu_done")
        sigmoid_done = signal("sigmoid_done")
        silu_step = signal("silu_step")
        inner_done = signal("inner_done")
        inner_hi = signal("inner_hi")
        inner_lo = signal("inner_lo")
        y_done = signal("y_done")
        y_added = signal("y_added")
        o_stats_done = signal("o_stats_done")
        o_mv_done = signal("o_mv_done")
        o_var_done = signal("o_var_done")
        o_rstd_step = signal("o_rstd_step")
        o_shift_done = signal("o_shift_done")
        xn_out_done = signal("xn_out_done")
        stored = signal("stored")
        xnt_stored = signal("xnt_stored")
        sp_own = signal("sp_own")
        dve_own = signal("dve_own")
        act_own = signal("act_own")

        IN_BANKS = [(0, 0), (1, 0), (0, 2), (1, 2)]
        OUT_BANKS = [(0, 0), (0, 1), (1, 0), (1, 1)]

        def xt_part(t, j):
            kt, e = IN_BANKS[j]
            return t[:, kt, e:e + 2].rearrange("p e c q -> p (e c q)")

        def xo_part(t, j):
            kt, c = OUT_BANKS[j]
            return t[:, kt, CH * c:CH * c + CH].rearrange("p (q e) -> p e q", e=E)

        def batches(eng, body):
            body(0)
            with eng.Fori(1, B - 1) as k:
                body(k)
            body(B - 1)

        def is_first(k):
            return isinstance(k, int) and k == 0

        def is_last(k):
            return isinstance(k, int) and k == B - 1

        def by_token(t, b):
            return t[b].rearrange("(c p e) d -> p c e d", c=NCH, e=E)

        def out_step(k):
            return 2 if is_last(k) else 1

        block = ctx.enter_context(nc.Block())

        @block.sync
        def _(sp):
            def load_residual(b, e):
                sp.dma_start(x_out[:, :, e], by_token(src, b)[:, :, e]).then_inc(res_in[e], 16)

            if post:
                sp.sem_inc(xnt_stored, XNT_STORED_CREDIT)
            for c in range(NCH):
                sp.dma_start(x_in[:, c], by_token(src, 0)[:, c]).then_inc(x_loaded[c], 16)
            sp.dma_start(idn[:, :], ident).then_inc(id_in, 16)
            for e in range(E):
                sp.dma_start(gu_raw[:, e], gate_up[e].rearrange("(k p) n -> p k n", p=P)).then_inc(w_in[e], 16)
                sp.dma_start(dn_raw[:, e], down[e].rearrange("(k p) n -> p k n", p=P)).then_inc(w_in[e], 16)
            for e in range(E):
                load_residual(0, e)

            def body(k):
                for e in range(E):
                    n = E * k + e
                    if post and e == out_step(k) + 1 and not is_first(k):
                        sp.wait_ge(xo_lo_done, 4 * k)
                        sp.sem_inc(sp_own, 1)
                        sp.dma_start(xnt[k - 1, 0], f(xo_hi[:, :, :])).then_inc(xnt_stored, 16)
                        sp.dma_start(xnt[k - 1, 1], f(xo_lo[:, :, :])).then_inc(xnt_stored, 16)
                    sp.wait_ge(y_added, n + 1)
                    sp.sem_inc(sp_own, 1)
                    sp.dma_start(by_token(dst, k)[:, :, e], x_out[:, :, e]).then_inc(stored, 16)
                    if not is_last(k):
                        sp.wait_ge(stored, 16 * n + 16)
                        if post:
                            sp.wait_ge(xn_out_done, n + 1)
                        sp.sem_inc(sp_own, 1)
                        load_residual(k + 1, e)

            batches(sp, body)
            sp.wait_ge(stored, 16 * B * E)
            for c in range(NCH):
                sp.wait_ge(x_loaded[c], 16 * (B + 2))
            if post:
                for j, (kt, c) in enumerate(OUT_BANKS):
                    sp.wait_ge(xo_lo_done, 4 * B - 3 + j)
                    toks = slice(CH * c, CH * c + CH)
                    sp.dma_start(xnt[B - 1, 0][:, kt, toks], f(xo_hi[:, kt, toks])).then_inc(xnt_stored, 16)
                    sp.dma_start(xnt[B - 1, 1][:, kt, toks], f(xo_lo[:, kt, toks])).then_inc(xnt_stored, 16)
                sp.wait_ge(xnt_stored, 32 * (B + 3) + XNT_STORED_CREDIT)

        @block.gpsimd
        def _(pool):
            pool.sem_inc(inner_lo, INNER_LO_CREDIT)
            pool.memset(mhalf[:, :], -0.5).then_inc(half_set, 1)
            pool.wait_ge(half_set, 1)

            def root(n, c):
                pool.wait_ge(var_done, 2 * n + c + 1)
                pool.tensor_tensor(rstd[:, c], var[:, c], mhalf[:, :], ALU.pow).then_inc(rstd_step, 1)
                pool.wait_ge(rstd_step, 2 * n + c + 1)
                pool.tensor_tensor(shift_in[:, c], minus_mean[:, c], rstd[:, c], ALU.mult).then_inc(shift_done, 1)

            def root_out(n, e):
                pool.wait_ge(o_var_done, n + 1)
                if not (isinstance(n, int) and n < 2):
                    pool.wait_ge(xn_out_done, n - 1)
                pool.tensor_tensor(o_rstd[:, e % 2], o_var[:, e % 2], mhalf[:, 0:NCH], ALU.pow).then_inc(o_rstd_step, 1)
                pool.wait_ge(o_rstd_step, n + 1)
                pool.tensor_tensor(o_shift[:, e % 2], o_minus_mean[:, e % 2], o_rstd[:, e % 2], ALU.mult).then_inc(o_shift_done, 1)

            def inner_low(n, e):
                pool.wait_ge(inner_hi, n + 1)
                pool.wait_ge(y_done, n - 1 + Y_DONE_CREDIT)
                pool.tensor_tensor(in_lo[:, e % 2].rearrange("p a b -> p (a b)"), inner[:, e % 2],
                                   f(in_hi[:, e % 2].rearrange("p a b -> p (a b)")), ALU.subtract).then_inc(inner_lo, 1)

            def split_down(e):
                pool.wait_ge(dn_hi_done, e + 1)
                pool.tensor_tensor(dn_lo[:, e], dn_raw[:, e], f(dn_hi[:, e]), ALU.subtract).then_inc(dn_lo_done, 1)

            def body(k):
                for e in range(E):
                    if post and not (is_first(k) and e == 0):
                        root_out(E * k + e - 1, (e - 1) % E)
                    if not (is_last(k) and e == E - 1):
                        inner_low(E * k + e + 1, (e + 1) % E)
                    if e in (0, 2) and not is_last(k):
                        root(k + 2, e // 2)

            for c in range(NCH):
                root(0, c)
            split_down(0)
            for c in range(NCH):
                root(1, c)
            inner_low(0, 0)
            for e in range(1, E):
                split_down(e)
            batches(pool, body)
            if post:
                root_out(E * B - 1, E - 1)

        @block.scalar
        def _(act):
            def split_gate_up(e):
                act.wait_ge(w_in[e], 32)
                act.activation(gu_hi[:, e], gu_raw[:, e], ACT.Copy).then_inc(gu_hi_done, 1)

            def split_down(e):
                act.activation(dn_hi[:, e], dn_raw[:, e], ACT.Copy).then_inc(dn_hi_done, 1)

            def normalise(n, c, used):
                act.wait_ge(shift_done, 2 * n + c + 1)
                if used is not None:
                    act.wait_ge(xt_turned, used)
                for e in range(E):
                    last = act.activation(xn[:, c, e], x_in[:, c, e], ACT.Identity, bias=shift_in[:, c, e:e + 1],
                                          scale=rstd[:, c, e:e + 1])
                last.then_inc(xn_done, 1)

            def fetch_input(b, c, n):
                act.wait_ge(xn_done, n)
                act.sem_inc(act_own, 1)
                act.dma_start(x_in[:, c], by_token(src, b)[:, c]).then_inc(x_loaded[c], 16)

            def normalise_out(n, e):
                act.wait_ge(o_shift_done, n + 1)
                for c in range(NCH):
                    last = act.activation(xn_out[:, c, e], x_out[:, c, e], ACT.Identity, bias=o_shift[:, e % 2, c:c + 1],
                                          scale=o_rstd[:, e % 2, c:c + 1])
                last.then_inc(xn_out_done, 1)

            def turn_in_hi(n, js):
                for j in js:
                    act.wait_ge(xt_turned, 4 * n + j + 1)
                    act.activation(xt_part(xt_hi, j), ps_t[:, j % 2], ACT.Copy).then_inc(xt_hi_done, 1)

            def turn_out_hi(k, js):
                for j in js:
                    act.wait_ge(xo_turned, 4 * k - 3 + j)
                    act.activation(xo_part(xo_hi, j), ps_t[:, j % 2], ACT.Copy).then_inc(xo_hi_done, 1)

            def sigmoid(n, e):
                act.wait_ge(gu_done, n + 1)
                act.wait_ge(inner_done, n - 1 + INNER_DONE_CREDIT)
                act.activation(sig[:, e % 2], ps_g[:, e % 2], ACT.Sigmoid).then_inc(sigmoid_done, 1)

            def inner_high(n, e):
                act.wait_ge(y_done, n - 1 + Y_DONE_CREDIT)
                act.wait_ge(inner_done, n + 1 + INNER_DONE_CREDIT)
                act.activation(in_hi[:, e % 2].rearrange("p a b -> p (a b)"), inner[:, e % 2],
                               ACT.Copy).then_inc(inner_hi, 1)

            def body(k):
                for e in range(E):
                    n = E * k + e
                    more = not (is_last(k) and e == E - 1)
                    if more:
                        sigmoid(n + 1, (e + 1) % E)
                    if e in (0, 2) and not is_last(k):
                        act.wait_ge(gu_done, E * k + e + 2)
                        turn_in_hi(k + 1, (e, e + 1))
                    if e == 3 and not is_last(k):
                        normalise(k + 2, 1, 4 * k + 8)
                    if post and e == out_step(k) and not is_first(k):
                        act.wait_ge(xnt_stored, 32 * k - 32 + XNT_STORED_CREDIT)
                        turn_out_hi(k, (0, 1))
                    if more:
                        inner_high(n + 1, (e + 1) % E)
                    if e == 3 and not is_last(k):
                        fetch_input((k + 3) % B, 1, 2 * k + 6)
                    if post and e == out_step(k):
                        if not is_first(k):
                            turn_out_hi(k, (2, 3))
                        for before in range(e):
                            normalise_out(E * k + before, before)
                    if e == 2 and not is_last(k):
                        normalise(k + 2, 0, 4 * k + 8)
                        fetch_input((k + 3) % B, 0, 2 * k + 5)
                    if post and not 0 < e <= out_step(k) and not (is_first(k) and e == 0):
                        normalise_out(n - 1, (e - 1) % E)

            normalise(0, 0, None)
            split_gate_up(0)
            fetch_input(1, 0, 1)
            split_down(0)
            fetch_input(1, 1, 2)
            turn_in_hi(0, range(4))
            for e in range(1, E):
                split_gate_up(e)
            sigmoid(0, 0)
            normalise(1, 0, 4)
            inner_high(0, 0)
            fetch_input(2, 0, 3)
            for e in range(1, E):
                split_down(e)
            fetch_input(2, 1, 4)
            batches(act, body)
            if post:
                normalise_out(E * B - 1, E - 1)
                act.wait_ge(xnt_stored, 32 * (B - 1) + XNT_STORED_CREDIT)
                turn_out_hi(B, range(4))

        @block.vector
        def _(dve):
            dve.sem_inc(inner_done, INNER_DONE_CREDIT)

            def input_stats(n, c):
                for e in range(E):
                    last = dve.bn_stats(stats[:, c, e], x_in[:, c, e])
                last.then_inc(stats_done, 1)

            def input_mean_var(n, c):
                dve.wait_ge(stats_done, 2 * n + c + 1)
                dve.sem_inc(dve_own, 1)
                for e in range(E):
                    last = dve.bn_aggr(mv[:, c, e], stats[:, c, e])
                last.then_inc(mv_done, 1)

            def input_moments(n, c):
                dve.wait_ge(mv_done, 2 * n + c + 1)
                dve.tensor_scalar(minus_mean[:, c], mv[:, c, :, 0], -1.0, None, ALU.mult)
                dve.tensor_scalar(var[:, c], mv[:, c, :, 1], EPS, None, ALU.add).then_inc(var_done, 1)

            def normalise_second(n):
                dve.wait_ge(shift_done, 2 * n + 2)
                for e in range(E):
                    if e == E - 1:
                        dve.wait_ge(xn_done, 2 * n + 1)
                    last = dve.tensor_scalar(xn[:, 1, e], x_in[:, 1, e], mv[:, 1, e, 0:1], rstd[:, 1, e:e + 1],
                                             ALU.subtract, ALU.mult)
                last.then_inc(xn_done, 1)

            def result_stats(n, e):
                dve.wait_ge(y_added, n + 1)
                dve.sem_inc(dve_own, 1)
                for c in range(NCH):
                    last = dve.bn_stats(o_stats[:, e % 2, c], x_out[:, c, e])
                last.then_inc(o_stats_done, 1)

            def result_mean_var(n, e):
                dve.wait_ge(o_stats_done, n + 1)
                dve.sem_inc(dve_own, 1)
                for c in range(NCH):
                    last = dve.bn_aggr(o_mv[:, e % 2, c], o_stats[:, e % 2, c])
                last.then_inc(o_mv_done, 1)

            def result_moments(n, e):
                dve.wait_ge(o_mv_done, n + 1)
                if not (isinstance(n, int) and n < 2):
                    dve.wait_ge(o_shift_done, n - 1)
                    dve.sem_inc(dve_own, 1)
                dve.tensor_scalar(o_minus_mean[:, e % 2], o_mv[:, e % 2, :, 0], -1.0, None, ALU.mult)
                dve.tensor_scalar(o_var[:, e % 2], o_mv[:, e % 2, :, 1], EPS, None, ALU.add).then_inc(o_var_done, 1)

            def turn_in_lo(n, js):
                for j in js:
                    dve.wait_ge(xt_hi_done, 4 * n + j + 1)
                    dve.tensor_tensor(xt_part(xt_lo, j), ps_t[:, j % 2], f(xt_part(xt_hi, j)),
                                      ALU.subtract).then_inc(xt_lo_done, 1)

            def turn_out_lo(k, js):
                for j in js:
                    dve.wait_ge(xo_hi_done, 4 * k - 3 + j)
                    dve.tensor_tensor(xo_part(xo_lo, j), ps_t[:, j % 2].rearrange("p (e q) -> p e q", q=P),
                                      f(xo_part(xo_hi, j)), ALU.subtract).then_inc(xo_lo_done, 1)

            def silu(n, e):
                dve.wait_ge(sigmoid_done, n + 1)
                dve.tensor_tensor(silu_g[:, e % 2], ps_g[:, e % 2], sig[:, e % 2], ALU.mult).then_inc(silu_step, 1)

            def make_inner(n, e):
                dve.wait_ge(silu_step, n + 1)
                dve.wait_ge(inner_lo, n - 1 + INNER_LO_CREDIT)
                dve.tensor_tensor(inner[:, e % 2], ps_u[:, e % 2], silu_g[:, e % 2], ALU.mult).then_inc(inner_done, 1)

            def add_y(n, k, e):
                dve.wait_ge(res_in[e], 16 * k + 16)
                dve.wait_ge(y_done, n + 1 + Y_DONE_CREDIT)
                dve.scalar_tensor_tensor(out=x_out[:, :, e], in0=ps_y[:, e % 2].rearrange("p (c d) -> p c d", c=NCH),
                                         scalar=0.5, in1=x_out[:, :, e], op0=ALU.mult, op1=ALU.add).then_inc(y_added, 1)

            def split_gate_up(e):
                dve.wait_ge(gu_hi_done, e + 1)
                dve.tensor_tensor(gu_lo[:, e], gu_raw[:, e], f(gu_hi[:, e]), ALU.subtract).then_inc(gu_lo_done, 1)

            def body(k):
                for e in range(E):
                    n = E * k + e
                    more = not (is_last(k) and e == E - 1)
                    before = post and not (is_first(k) and e == 0)
                    if more:
                        silu(n + 1, (e + 1) % E)
                    if before:
                        result_mean_var(n - 1, (e - 1) % E)
                    if more:
                        make_inner(n + 1, (e + 1) % E)
                    if before:
                        result_moments(n - 1, (e - 1) % E)
                    chunk = e // 2 if e in (0, 2) and not is_last(k) else None
                    if chunk is not None:
                        dve.wait_ge(x_loaded[chunk], 16 * k + 48)
                        dve.sem_inc(dve_own, 1)
                        input_stats(k + 2, chunk)
                        turn_in_lo(k + 1, (e,))
                        input_mean_var(k + 2, chunk)
                        turn_in_lo(k + 1, (e + 1,))
                        input_moments(k + 2, chunk)
                    if post and e == out_step(k) and not is_first(k):
                        turn_out_lo(k, (0, 1))
                    add_y(n, k, e)
                    if post:
                        result_stats(n, e)
                        if e == out_step(k) and not is_first(k):
                            turn_out_lo(k, (2, 3))

            for c in range(NCH):
                dve.wait_ge(x_loaded[c], 16)
                input_stats(0, c)
                input_mean_var(0, c)
                input_moments(0, c)
            normalise_second(0)
            split_gate_up(0)
            turn_in_lo(0, range(4))
            for c in range(NCH):
                split_gate_up(1 + c)
                dve.wait_ge(x_loaded[c], 32)
                input_stats(1, c)
                input_mean_var(1, c)
                dve.wait_ge(shift_done, c + 1)
                input_moments(1, c)
            split_gate_up(3)
            silu(0, 0)
            make_inner(0, 0)
            normalise_second(1)
            batches(dve, body)
            if post:
                result_mean_var(E * B - 1, E - 1)
                result_moments(E * B - 1, E - 1)
                turn_out_lo(B, range(4))

        @block.tensor
        def _(pe):
            pe.sem_inc(y_done, Y_DONE_CREDIT)

            def turn_in(n, js, freed):
                pe.wait_ge(xn_done, 2 * n + 2)
                for j in js:
                    if freed is not None:
                        pe.wait_ge(freed[0], freed[1] + j % 2)
                    elif j >= 2:
                        pe.wait_ge(xt_lo_done, j - 1)
                    kt, e0 = IN_BANKS[j]
                    for i in range(4):
                        e, c = e0 + i // 2, i % 2
                        last = pe.transpose(ps_t[:, j % 2, P * i:P * i + P], xn[:, c, e, P * kt:P * kt + P], idn[:, :])
                    last.then_inc(xt_turned, 1)

            def turn_out(k, js, freed):
                pe.wait_ge(xn_out_done, E * k)
                for j in js:
                    if j < 2:
                        pe.wait_ge(freed[0], freed[1] + j)
                    else:
                        pe.wait_ge(xo_lo_done, 4 * k - 5 + j)
                    kt, c = OUT_BANKS[j]
                    for e in range(E):
                        last = pe.transpose(ps_t[:, j % 2, P * e:P * e + P], xn_out[:, c, e, P * kt:P * kt + P], idn[:, :])
                    last.then_inc(xo_turned, 1)

            def gate_up_of(n, e, turned_before):
                pe.wait_ge(xt_lo_done, turned_before)
                pe.wait_ge(inner_done, n - 1 + INNER_DONE_CREDIT)
                for out, col in ((ps_g, 0), (ps_u, I)):
                    for m in range(2):
                        j = 0
                        for kt in range(KT):
                            cols = slice(col + P * m, col + P * m + P)
                            x_h = xt_hi[:, kt, e].rearrange("p c q -> p (c q)")
                            x_l = xt_lo[:, kt, e].rearrange("p c q -> p (c q)")
                            for w, x in passes(gu_hi[:, e, kt, cols], gu_lo[:, e, kt, cols], x_h, x_l):
                                last = pe.matmul(out[:, e % 2, D * m:D * m + D], w, x, start=j == 0, stop=j == 3 * KT - 1)
                                j += 1
                last.then_inc(gu_done, 1)

            def down_of(n, e):
                pe.wait_ge(inner_lo, n + 1 + INNER_LO_CREDIT)
                if not (isinstance(n, int) and n < 2):
                    pe.wait_ge(y_added, n - 1)
                for c in range(NCH):
                    j = 0
                    for m in range(2):
                        i_h, i_l = in_hi[:, e % 2, m, P * c:P * c + P], in_lo[:, e % 2, m, P * c:P * c + P]
                        for i, w in passes(i_h, i_l, dn_hi[:, e, m], dn_lo[:, e, m]):
                            last = pe.matmul(ps_y[:, e % 2, D * c:D * c + D], i, w, start=j == 0, stop=j == 5)
                            j += 1
                last.then_inc(y_done, 1)

            def body(k):
                for e in range(E):
                    n = E * k + e
                    if e < 2:
                        if is_first(k):
                            pe.wait_ge(gu_lo_done, e + 3)
                        gate_up_of(n + 2, e + 2, 4 * k + 4)
                    elif not is_last(k):
                        gate_up_of(n + 2, e - 2, 4 * k + 6)
                    if e in (0, 2) and not is_last(k):
                        after_out = post and e == 2 and not is_first(k)
                        turn_in(k + 1, (e, e + 1), (xo_lo_done, 4 * k - 1) if after_out else (xt_lo_done, 4 * k + 3 + e))
                    if post and e == out_step(k) and not is_first(k):
                        turn_out(k, (0, 1), (xt_lo_done, 4 * k + 3 if is_last(k) else 4 * k + 5))
                    if is_first(k):
                        pe.wait_ge(dn_lo_done, e + 1)
                    down_of(n, e)
                    if post and e == out_step(k) and not is_first(k):
                        turn_out(k, (2, 3), None)

            pe.wait_ge(id_in, 16)
            turn_in(0, range(4), None)
            for e in range(2):
                pe.wait_ge(gu_lo_done, e + 1)
                gate_up_of(e, e, 4)
            batches(pe, body)
            if post:
                turn_out(B, range(4), (xo_lo_done, 4 * B - 5))


STEPS = 2 * NT


def chunks(s):
    h, i = divmod(s, NT)
    first = 12 * h + (i if i < 4 else 4 + 2 * (i - 4))
    return [(first + c, c, min(CH, P * (i + 1) - CH * c)) for c in range(i // 4 + 1)]


NCHUNK = sum(len(chunks(s)) for s in range(STEPS))
QK_ORDER = [("q", 0), ("q", 1), ("k", 0), ("k", 1), ("q", 2), ("q", 3), ("k", 2), ("k", 3)]
QKV_ORDER = QK_ORDER + [("v", 0), ("v", 1), ("v", 2), ("v", 3)]
QKV_FILLS = dict(zip((0, 2, 3, 4, 6, 7, 8, 10, 11, 12, 14, 15), QKV_ORDER))
OUT_FILLS = {0: 0, 2: 1, 5: 2, 6: 3, 9: 4, 11: 5, 12: 6, 13: 7}
FILLS = []
for _s in range(STEPS):
    if _s in QKV_FILLS:
        FILLS.append(QKV_FILLS[_s])
    if _s in OUT_FILLS:
        FILLS.append(("o", OUT_FILLS[_s]))
WEIGHTS = [(2, "v"), (7, "o"), (9, "q"), (12, "k")]
W_INDEX = {w: n for n, (_, w) in enumerate(WEIGHTS)}
W_FIRST = ["q", "k", "v", "q", "k"]
W_BEFORE = len(W_FIRST)
QK_SPLITS = [(0, 0, 1, 0, 0), (2, 0, 1, 1, 0), (2, 0, 1, 0, 1), (6, 0, 1, 1, 1),
             (8, 1, 0, 0, 0), (10, 1, 0, 1, 0), (15, 1, 0, 0, 1), (15, 1, 0, 1, 1)]
QK_BEFORE = 4
LATE_PRODUCTS = (4,)
EARLY_CONTEXT = (7, 15)
RDEN_BEFORE = 1


def bank(kind, idx, m, final=False):
    if final:
        return idx % 2
    if isinstance(m, int) and m == 0:
        return idx % 2
    return FILLS.index((kind, idx)) % 2


def attention_stage(nc, src, dst, xnt, wq, wk, wv, wo, rope, mask, ident):
    with ExitStack() as ctx:
        def sb(name, shape, dt=F32):
            return ctx.enter_context(nc.sbuf_tensor(name, shape, dt))

        def ps(name, shape):
            return ctx.enter_context(nc.psum_tensor(name, shape, F32))

        def signal(name):
            return ctx.enter_context(nc.semaphore(name))

        raw = {w: sb(f"raw_{w}", [P, KT, 2 * HD]) for w in "qkvo"}
        w_hi = {w: sb(f"w_hi_{w}", [P, KT, 2 * HD], F32R) for w in "qkvo"}
        w_lo = {w: sb(f"w_lo_{w}", [P, KT, 2 * HD], F32R) for w in "qkvo"}
        xt_hi = sb("xt_hi", [P, KT, S], F32R)
        xt_lo = sb("xt_lo", [P, KT, S], F32R)
        x = sb("x", [P, NT, D])
        cs = sb("cs", [P, 4, 2, 256])
        msk = sb("msk", [P, P])
        idn = sb("idn", [P, P])
        prod_a = sb("prod_a", [P, 2, 2, 256])
        prod_b = sb("prod_b", [P, 2, 2, 256])
        rot2 = sb("rot2", [P, 2, CH])
        qk_raw = sb("qk_raw", [P, 2, 2, S])
        qk_hi = sb("qk_hi", [P, 2, 2, S], F32R)
        qk_lo = sb("qk_lo", [P, 2, 2, S], F32R)
        v_raw = sb("v_raw", [P, NT, 2 * HD])
        v_hi = sb("v_hi", [P, NT, 2 * HD], F32R)
        v_lo = sb("v_lo", [P, NT, 2 * HD], F32R)
        probs = sb("probs", [P, 2, S])
        pt_hi = [sb(f"pt_hi{c}", [P, 4 * (c + 1), CH], F32R) for c in range(2)]
        pt_lo = [sb(f"pt_lo{c}", [P, 4 * (c + 1), CH], F32R) for c in range(2)]
        ctx_hi = sb("ctx_hi", [P, CH], F32R)
        ctx_lo = sb("ctx_lo", [P, CH], F32R)
        part_max = sb("part_max", [P, 2, 4])
        neg_max = sb("neg_max", [P, 4])
        den = sb("den", [P, 2, NT, 2])
        den_sum = sb("den_sum", [P, 2, NT])
        rden = sb("rden", [P, 2, NT])
        ps_s = ps("ps_s", [P, 3, CH])
        ps_t = ps("ps_t", [P, 2, CH])
        ps_c = ps("ps_c", [P, CH])
        ps_f = ps("ps_f", [P, 2, CH])

        rope_in = signal("rope_in")
        const_in = signal("const_in")
        raw_in = {w: signal(f"raw_in_{w}") for w in "qkvo"}
        q_scaled = signal("q_scaled")
        w_hi_done = signal("w_hi_done")
        w_lo_done = signal("w_lo_done")
        xt_in = [signal(f"xt_in{half}") for half in range(2)]
        x_in = [signal(f"x_in{c}") for c in range(2)]
        x_out = [signal(f"x_out{c}") for c in range(2)]
        zeroed = signal("zeroed")
        qk_filled = signal("qk_filled")
        v_filled = signal("v_filled")
        out_filled = signal("out_filled")
        prod_done = signal("prod_done")
        rot_done = signal("rot_done")
        parted = signal("parted")
        shifted = [signal(f"shifted{g}") for g in range(4)]
        qk_hi_done = signal("qk_hi_done")
        qk_lo_done = signal("qk_lo_done")
        v_raw_done = signal("v_raw_done")
        v_hi_done = signal("v_hi_done")
        v_lo_done = signal("v_lo_done")
        scored = signal("scored")
        part_done = signal("part_done")
        max_done = signal("max_done")
        exp_done = signal("exp_done")
        p_turned = signal("p_turned")
        pt_hi_done = signal("pt_hi_done")
        pt_lo_done = signal("pt_lo_done")
        pv_done = signal("pv_done")
        ctx_hi_done = signal("ctx_hi_done")
        ctx_lo_done = signal("ctx_lo_done")
        den_summed = signal("den_summed")
        rden_done = signal("rden_done")
        out_added = signal("out_added")
        sp_own = signal("sp_own")
        dve_own = signal("dve_own")

        def batches(eng, body):
            with eng.Fori(0, B - 1) as b:
                with eng.Fori(0, PAIRS - 1) as p:
                    body(b * PAIRS + p, b, "middle")
                body(b * PAIRS + PAIRS - 1, b, "last")
            with eng.Fori(0, PAIRS - 1) as p:
                body((B - 1) * PAIRS + p, B - 1, "middle")
            body(NPAIR - 1, B - 1, "final")

        def weights_of(kind):
            return [(step, w, at) for at, (step, w) in enumerate(WEIGHTS if kind != "final" else WEIGHTS[1:2])]

        def ends(s, kind):
            return kind == "final" and s == STEPS - 1

        def weight_view(t, w):
            return t[:, :, :].rearrange("p k (two f) -> p k two f", two=2) if w in "qk" else t[:, :, :]

        def raw_view(w):
            return raw[w][:, :, :].rearrange("p k (f two) -> p k two f", two=2) if w in "qk" else raw[w][:, :, :]

        block = ctx.enter_context(nc.Block())

        @block.sync
        def _(sp):
            w_dram = {"q": wq, "k": wk, "v": wv}

            def load_raw(w, pair):
                if w == "o":
                    view = wo[bass.ds(pair * 2 * HD, 2 * HD), :].rearrange("(h p) d -> p h d", p=P)
                else:
                    view = w_dram[w][:, bass.ds(pair * 2 * HD, 2 * HD)].rearrange("(k p) n -> p k n", p=P)
                sp.dma_start(raw[w][:, :, :], view).then_inc(raw_in[w], 16)

            def load_xt(batch, half):
                toks = slice(CH * half, CH * half + CH)
                sp.dma_start(f(xt_hi[:, :, toks]), xnt[batch, 0][:, :, toks]).then_inc(xt_in[half], 16)
                sp.dma_start(f(xt_lo[:, :, toks]), xnt[batch, 1][:, :, toks]).then_inc(xt_in[half], 16)

            def shift(m, g):
                sp.wait_ge(rot_done, 8 * m + 2 * g + 2)
                sp.sem_inc(sp_own, 1)
                kind, cols = g % 2, slice(CH * (g // 2), CH * (g // 2) + CH)
                sp.dma_start(qk_raw[HALF:P, kind, 1, cols], qk_raw[HALF:P, kind, 0, cols]).then_inc(parted, 16)
                sp.dma_start(qk_raw[0:HALF, kind, 1, cols], rot2[HALF:P, g % 2]).then_inc(shifted[g], 16)
                sp.wait_ge(parted, 16 * (4 * m + g + 1))
                sp.sem_inc(sp_own, 1)
                sp.dma_start(qk_raw[HALF:P, kind, 0, cols], rot2[0:HALF, g % 2]).then_inc(shifted[g], 16)

            def rows(t, b, c):
                return t[b].rearrange("(t p) d -> p t d", p=P)[:, 4 * c:4 * c + 4]

            def turn_over_x(n, b, c, store):
                sp.wait_ge(out_added, 8 * n + 2 * c + 2 + OUT_ADDED_CREDIT)
                sp.sem_inc(sp_own, 1)
                if store:
                    sp.dma_start(rows(dst, b - 1, c), x[:, 4 * c:4 * c + 4]).then_inc(x_out[c], 16)
                    sp.wait_ge(x_out[c], 16 * b)
                    sp.sem_inc(sp_own, 1)
                sp.dma_start(x[:, 4 * c:4 * c + 4], rows(src, b, c)).then_inc(x_in[c], 16)

            def body(n, b, p, kind, store=True):
                if kind == "final":
                    return

                def next_raw(w, at):
                    sp.wait_ge(w_lo_done, W_BEFORE + 4 * n + W_INDEX[w] + 1)
                    sp.sem_inc(sp_own, 1)
                    load_raw(w, (p + at) % PAIRS)

                if kind == "last":
                    for half in range(2):
                        sp.wait_ge(v_filled, 4 * n + 2 * half + 2)
                        sp.sem_inc(sp_own, 1)
                        load_xt((b + 1) % B, half)
                for s in range(STEPS):
                    if s in QKV_FILLS and QKV_FILLS[s][0] != "v" and QK_ORDER.index(QKV_FILLS[s]) % 2:
                        shift(n + 1, QK_ORDER.index(QKV_FILLS[s]) // 2)
                    for step, w in WEIGHTS:
                        if step == s:
                            next_raw(w, {"v": 2, "o": 1, "q": 3, "k": 3}[w])
                    if kind == "first" and OUT_FILLS.get(s) in (1, 3):
                        turn_over_x(n, b, OUT_FILLS[s] // 2, store)

            def batch(b, store, end="last"):
                body(b * PAIRS, b, 0, "first", store)
                with sp.Fori(1, PAIRS - 1) as p:
                    body(b * PAIRS + p, b, p, "middle")
                body(b * PAIRS + PAIRS - 1, b, PAIRS - 1, end)

            load_raw("q", 0)
            load_raw("k", 0)
            load_xt(0, 0)
            sp.dma_start(cs[:, :, :, :], rope).then_inc(rope_in, 16)
            load_raw("v", 0)
            load_xt(0, 1)
            sp.dma_start(msk[:, :], mask).then_inc(const_in, 16)
            sp.dma_start(idn[:, :], ident).then_inc(const_in, 16)
            load_raw("o", 0)
            for n, w in enumerate(W_FIRST[:3]):
                sp.wait_ge(w_lo_done, n + 1)
                load_raw(w, 1)
            for g in range(4):
                shift(0, g)
            for n, w in enumerate(W_FIRST[3:]):
                sp.wait_ge(w_lo_done, 3 + n + 1)
                load_raw(w, 2)
            batch(0, False)
            with sp.Fori(1, B - 1) as b:
                batch(b, True)
            batch(B - 1, True, "final")
            for c in range(2):
                sp.wait_ge(out_added, 8 * NPAIR + 2 * c + 2 + OUT_ADDED_CREDIT)
                sp.dma_start(rows(dst, B - 1, c), x[:, 4 * c:4 * c + 4]).then_inc(x_out[c], 16)
            for c in range(2):
                sp.wait_ge(x_out[c], 16 * B)
            for w in "qkvo":
                sp.wait_ge(raw_in[w], 16 * (NPAIR + {"q": 2, "k": 2, "v": 1, "o": 0}[w]))

        @block.gpsimd
        def _(pool):
            def weight_lo(w, count, used, n_used):
                pool.wait_ge(w_hi_done, count)
                if used is not None:
                    pool.wait_ge(used, n_used)
                pool.tensor_tensor(weight_view(w_lo[w], w), raw_view(w), weight_view(f(w_hi[w][:, :, :]), w),
                                   ALU.subtract).then_inc(w_lo_done, 1)

            def rotate(m, idx):
                g = idx // 2
                kind, t = "qk".index(QK_ORDER[idx][0]), QK_ORDER[idx][1]
                cols = slice(256 * t, 256 * t + 256)
                pool.wait_ge(prod_done, 8 * m + idx + 1)
                if idx % 2 == 0 and not isinstance(m, int):
                    pool.wait_ge(qk_lo_done, QK_BEFORE + 8 * (m - 1) + g + 1)
                if idx % 2 == 0:
                    before = 32 * (m + 1) if g >= 2 else 32 * m
                    if not (isinstance(before, int) and before == 0):
                        pool.wait_ge(shifted[(g + 2) % 4], before)
                pool.tensor_tensor(qk_raw[:, kind, 0, cols], prod_a[:, idx % 2, 0], prod_a[:, idx % 2, 1], ALU.subtract)
                pool.tensor_tensor(rot2[:, g % 2, 256 * (t % 2):256 * (t % 2) + 256], prod_b[:, idx % 2, 0],
                                   prod_b[:, idx % 2, 1], ALU.add).then_inc(rot_done, 1)

            def qk_low(count, h, kind, half):
                toks = slice(CH * half, CH * half + CH)
                pool.wait_ge(qk_hi_done, count)
                pool.tensor_tensor(qk_lo[:, kind, h, toks], qk_raw[:, kind, h, toks], f(qk_hi[:, kind, h, toks]),
                                   ALU.subtract).then_inc(qk_lo_done, 1)

            def v_low(m, h):
                pool.wait_ge(v_hi_done, 2 * m + h + 1)
                cols = slice(HD * h, HD * h + HD)
                pool.tensor_tensor(v_lo[:, :, cols], v_raw[:, :, cols], f(v_hi[:, :, cols]),
                                   ALU.subtract).then_inc(v_lo_done, 1)

            def body(n, b, kind_of_body):
                for s in range(STEPS):
                    for j, (step, ahead, h, kind, half) in enumerate(QK_SPLITS):
                        if step == s and not (kind_of_body == "final" and ahead):
                            qk_low(QK_BEFORE + 8 * n + j + 1, h, kind, half)
                    if s in QKV_FILLS and QKV_FILLS[s][0] != "v" and kind_of_body != "final":
                        rotate(n + 1, QK_ORDER.index(QKV_FILLS[s]))
                    if s == 1:
                        v_low(n, 0)
                    if s == 5:
                        v_low(n, 1)
                    for step, w, idx in weights_of(kind_of_body):
                        if step == s:
                            used, count = {"v": (v_filled, 4 * n + 4), "o": (out_filled, 8 * n + 4 + OUT_FILLED_CREDIT),
                                           "q": (qk_filled, 8 * n + 14), "k": (qk_filled, 8 * n + 16)}[w]
                            weight_lo(w, W_BEFORE + 4 * n + idx + 1, used, count)

            for n, w in enumerate(W_FIRST):
                if n == 3:
                    for idx in range(8):
                        rotate(0, idx)
                    for j in range(4):
                        qk_low(j + 1, 0, j % 2, j // 2)
                weight_lo(w, n + 1, qk_filled if n >= 3 else None, 8)
            batches(pool, body)

        @block.scalar
        def _(act):
            def v_copy(m, idx):
                act.wait_ge(v_filled, 4 * m + idx + 1)
                act.activation(v_raw[:, 2 * idx:2 * idx + 2].rearrange("p t d -> p (t d)"), ps_f[:, bank("v", idx, m)],
                               ACT.Copy).then_inc(v_raw_done, 1)

            def qk_high(m, h, kind, half, n_scored):
                g = 2 * half + kind
                toks = slice(CH * half, CH * half + CH)
                act.wait_ge(rot_done, 8 * m + 2 * g + 2)
                act.wait_ge(shifted[g], 32 * (m + 1))
                if n_scored is not None:
                    act.wait_ge(scored, n_scored)
                act.activation(qk_hi[:, kind, h, toks], qk_raw[:, kind, h, toks], ACT.Copy).then_inc(qk_hi_done, 1)

            def v_high(m, h, sig, n):
                act.wait_ge(v_raw_done, 4 * m + 4)
                act.wait_ge(sig, n)
                cols = slice(HD * h, HD * h + HD)
                act.activation(v_hi[:, :, cols], v_raw[:, :, cols], ACT.Copy).then_inc(v_hi_done, 1)

            def exps(n, s, slot_used=True):
                act.wait_ge(max_done, STEPS * n + s + 1)
                if slot_used:
                    before = chunks(s - 2)[-1][0] if s >= 2 else chunks(s - 2 + STEPS)[-1][0] - NCHUNK
                    act.wait_ge(p_turned, NCHUNK * n + before + 1 + P_TURNED_CREDIT)
                h, i = divmod(s, NT)
                for ci, c, k in chunks(s):
                    act.activation(probs[:, s % 2, CH * c:CH * c + k], ps_s[:, ci % 3, 0:k], ACT.Exp,
                                   bias=neg_max[:, s % 4:s % 4 + 1],
                                   accum_out=den[:, h, i, c:c + 1]).then_inc(exp_done, 1)

            def pt_high(n, s, ci, c, k):
                i = s % NT
                act.wait_ge(p_turned, NCHUNK * n + ci + 1 + P_TURNED_CREDIT)
                act.activation(pt_hi[i // 4][:, 4 * c:4 * c + k // P, P * (i % 4):P * (i % 4) + P],
                               ps_t[:, ci % 2, 0:k].rearrange("p (j q) -> p j q", q=P), ACT.Copy).then_inc(pt_hi_done, 1)

            def ctx_high(n, k):
                act.wait_ge(pv_done, 4 * n + k + 1)
                act.wait_ge(out_filled, 8 * n + 2 * k + 2 + OUT_FILLED_CREDIT)
                act.activation(ctx_hi[:, :], ps_c[:, :], ACT.Copy).then_inc(ctx_hi_done, 1)

            def body(n, b, kind_of_body):
                for s in range(STEPS):
                    if s in QKV_FILLS and QKV_FILLS[s][0] == "v" and kind_of_body != "final":
                        if QKV_FILLS[s][1] == 0:
                            act.wait_ge(v_lo_done, 2 * n + 2)
                        v_copy(n + 1, QKV_FILLS[s][1])
                    m, nxt = (n, s + 1) if s + 1 < STEPS else (n + 1, 0)
                    if len(chunks(nxt)) == 1 and not ends(s, kind_of_body):
                        exps(m, nxt)
                    for ci, c, k in chunks(s):
                        if c and s in EARLY_CONTEXT:
                            ctx_high(n, s // 4)
                        pt_high(n, s, ci, c, k)
                    if s % 4 == 3 and s not in EARLY_CONTEXT:
                        ctx_high(n, s // 4)
                    if len(chunks(nxt)) > 1:
                        exps(m, nxt)
                    for step, w, _ in weights_of(kind_of_body):
                        if step == s:
                            if w == "q":
                                act.wait_ge(q_scaled, n + 3)
                            else:
                                act.wait_ge(raw_in[w], 16 * n + {"v": 32, "o": 16, "k": 48}[w])
                            used, count = {"v": (v_filled, 4 * n + 4), "o": (out_filled, 8 * n + 4 + OUT_FILLED_CREDIT),
                                           "q": (qk_filled, 8 * n + 14), "k": (qk_filled, 8 * n + 16)}[w]
                            act.wait_ge(used, count)
                            act.activation(weight_view(w_hi[w], w), raw_view(w), ACT.Copy).then_inc(w_hi_done, 1)
                    for step, ahead, h, kind, half in QK_SPLITS:
                        if step == s and not (kind_of_body == "final" and ahead):
                            qk_high(n + ahead, h, kind, half, NCHUNK * n + (NCHUNK // 2 if ahead else 1))
                    if s == 1:
                        v_high(n, 0, p_turned, NCHUNK * n + 1 + P_TURNED_CREDIT)
                    if s == 5:
                        v_high(n, 1, pv_done, 4 * n + 1)

            act.sem_inc(exp_done, EXP_DONE_CREDIT)
            for n, w in enumerate(W_FIRST):
                if n == 3:
                    for half in range(2):
                        for idx in range(2 * half, 2 * half + 2):
                            v_copy(0, idx)
                        for kind in range(2):
                            qk_high(0, 0, kind, half, None)
                    act.wait_ge(qk_filled, 8)
                if w == "q":
                    act.wait_ge(q_scaled, 1 + n // 3)
                else:
                    act.wait_ge(raw_in[w], 16 + 16 * (n // 3))
                act.activation(weight_view(w_hi[w], w), raw_view(w), ACT.Copy).then_inc(w_hi_done, 1)
            exps(0, 0, False)
            batches(act, body)
            ctx_high(NPAIR, 0)

        @block.vector
        def _(dve):
            def scale_q(m):
                dve.wait_ge(raw_in["q"], 16 * (m + 1))
                dve.tensor_scalar(raw["q"][:, :, :], raw["q"][:, :, :], float(1.0 / np.sqrt(HD)), None,
                                  ALU.mult).then_inc(q_scaled, 1)

            def products(m, idx):
                kind, t = QK_ORDER[idx]
                pair = ps_f[:, bank(kind, t, m)].rearrange("p (a n) -> p a n", a=2)
                dve.wait_ge(qk_filled, 8 * m + idx + 1)
                before = 8 * m + idx - 1
                if not (isinstance(before, int) and before <= 0):
                    dve.wait_ge(rot_done, before)
                dve.tensor_tensor(prod_a[:, idx % 2], pair, cs[:, t], ALU.mult)
                dve.tensor_tensor(prod_b[:, idx % 2], pair, cs[:, t, ::-1], ALU.mult).then_inc(prod_done, 1)

            parts = [0]
            for s in range(STEPS):
                i = s % NT
                parts.append(parts[-1] + (1 if i == 0 else 2 if i <= 4 else 3))

            def part_maxima(n, s, which):
                i = s % NT
                ci, c, k = chunks(s)[which]
                at = which
                dve.wait_ge(scored, NCHUNK * n + ci + 1)
                if c == i // 4:
                    dve.sem_inc(dve_own, 1)
                    own = ps_s[:, ci % 3, k - P:k]
                    dve.tensor_tensor_reduce(own, own, msk[:, :], 1.0, -3e38, ALU.add, ALU.max,
                                             part_max[:, s % 2, at:at + 1]).then_inc(part_done, 1)
                    at += 1
                    k -= P
                if k:
                    dve.tensor_reduce(part_max[:, s % 2, at:at + 1], ps_s[:, ci % 3, 0:k], AX.X, ALU.max)\
                       .then_inc(part_done, 1)
                    at += 1
                if c == i // 4:
                    dve.wait_ge(part_done, parts[STEPS] * n + parts[s] + at)
                    dve.tensor_reduce(neg_max[:, s % 4:s % 4 + 1], part_max[:, s % 2, 0:at], AX.X, ALU.max,
                                      negate=True).then_inc(max_done, 1)

            def pt_low(n, s, ci, c, k):
                i = s % NT
                at = (slice(4 * c, 4 * c + k // P), slice(P * (i % 4), P * (i % 4) + P))
                dve.wait_ge(pt_hi_done, NCHUNK * n + ci + 1)
                dve.tensor_tensor(pt_lo[i // 4][:, at[0], at[1]], ps_t[:, ci % 2, 0:k].rearrange("p (j q) -> p j q", q=P),
                                  f(pt_hi[i // 4][:, at[0], at[1]]), ALU.subtract).then_inc(pt_lo_done, 1)

            def ctx_low(n, k):
                dve.wait_ge(ctx_hi_done, 4 * n + k + 1)
                dve.tensor_tensor(ctx_lo[:, :], ps_c[:, :], f(ctx_hi[:, :]), ALU.subtract).then_inc(ctx_lo_done, 1)

            def reciprocal(n, r):
                h, c = divmod(r, 2)
                blocks = slice(4 * c, 4 * c + 4)
                dve.wait_ge(exp_done, NCHUNK * n + chunks(NT * h + 4 * c + 3)[-1][0] + 1 + EXP_DONE_CREDIT)
                if c:
                    dve.tensor_tensor(den_sum[:, h, blocks], den[:, h, blocks, 0], den[:, h, blocks, 1],
                                      ALU.add).then_inc(den_summed, 1)
                    dve.wait_ge(den_summed, 2 * n + h + 1)
                    dve.reciprocal(rden[:, h, blocks], den_sum[:, h, blocks]).then_inc(rden_done, 1)
                else:
                    dve.reciprocal(rden[:, h, blocks], den[:, h, blocks, 0]).then_inc(rden_done, 1)

            def add_out(n, w, final):
                h = 1 if w < 4 else 0
                dve.wait_ge(out_filled, 8 * n + w + 1 + OUT_FILLED_CREDIT)
                for u in range(2):
                    t = 4 * (w // 2 % 2) + 2 * (w % 2) + u
                    last = dve.scalar_tensor_tensor(out=x[:, t], in0=ps_f[:, bank("o", w, n, final), D * u:D * u + D],
                                                    scalar=rden[:, h, t:t + 1], in1=x[:, t], op0=ALU.mult, op1=ALU.add)
                last.then_inc(out_added, 1)

            def body(n, b, kind_of_body):
                for s in range(STEPS):
                    m, nxt = (n, s + 1) if s + 1 < STEPS else (n + 1, 0)
                    if s == 7 and kind_of_body != "final":
                        scale_q(n + 2)
                    if not ends(s, kind_of_body):
                        part_maxima(m, nxt, 0)
                    if s in QKV_FILLS and QKV_FILLS[s][0] != "v" and s not in LATE_PRODUCTS and kind_of_body != "final":
                        products(n + 1, QK_ORDER.index(QKV_FILLS[s]))
                    work = chunks(s)
                    pt_low(n, s, *work[0])
                    if len(chunks(nxt)) > 1:
                        part_maxima(m, nxt, 1)
                    if s in EARLY_CONTEXT:
                        ctx_low(n, s // 4)
                    if len(work) > 1:
                        pt_low(n, s, *work[1])
                    if s in OUT_FILLS:
                        w = OUT_FILLS[s]
                        if w % 2 == 0:
                            dve.wait_ge(rden_done, 4 * n + w // 2 - 1 + RDEN_BEFORE)
                        if w in (4, 6):
                            dve.wait_ge(x_in[w // 2 - 2], 16 * b + 16)
                        add_out(n, w, kind_of_body == "final")
                    if s % 4 == 3 and s not in EARLY_CONTEXT:
                        ctx_low(n, s // 4)
                    if s in (4, 8, 12, 15):
                        reciprocal(n, {4: 0, 8: 1, 12: 2, 15: 3}[s])
                    if s in QKV_FILLS and QKV_FILLS[s][0] != "v" and s in LATE_PRODUCTS and kind_of_body != "final":
                        products(n + 1, QK_ORDER.index(QKV_FILLS[s]))

            scale_q(0)
            for t in (pt_hi[1][:, :, :], pt_lo[1][:, :, :]):
                dve.memset(f(t), 0.0).then_inc(zeroed, 1)
            dve.memset(rden[:, :, :], 0.0).then_inc(rden_done, RDEN_BEFORE)
            dve.sem_inc(pt_lo_done, PT_LO_DONE_CREDIT)
            dve.sem_inc(ctx_lo_done, CTX_LO_DONE_CREDIT)
            dve.sem_inc(out_added, OUT_ADDED_CREDIT)
            dve.wait_ge(rope_in, 16)
            for idx in range(8):
                products(0, idx)
            scale_q(1)
            for t in (v_hi[:, :, HD:], v_lo[:, :, HD:], ctx_hi[:, :], ctx_lo[:, :], w_hi["o"][:, :, :], w_lo["o"][:, :, :]):
                dve.memset(f(t), 0.0).then_inc(zeroed, 1)
            dve.memset(x[:, :, :], 0.0).then_inc(zeroed, 1)
            dve.wait_ge(const_in, 32)
            part_maxima(0, 0, 0)
            batches(dve, body)
            add_out(NPAIR, 0, True)
            add_out(NPAIR, 1, True)
            ctx_low(NPAIR, 0)
            add_out(NPAIR, 2, True)
            add_out(NPAIR, 3, True)

        @block.tensor
        def _(pe):
            def bank_free(n, kind, idx):
                at = FILLS.index((kind, idx)) - 2
                before, j = FILLS[at]
                back = 1 if at < 0 else 0
                if before == "o":
                    pe.wait_ge(out_added, 8 * (n - back) + j + 1 + OUT_ADDED_CREDIT)
                elif before == "v":
                    pe.wait_ge(v_raw_done, 4 * (n + 1 - back) + j + 1)
                else:
                    pe.wait_ge(prod_done, 8 * (n + 1 - back) + QK_ORDER.index((before, j)) + 1)

            def fill(m, kind, idx):
                out = ps_f[:, bank(kind, idx, m)]
                if kind == "v":
                    for u in range(2):
                        t = 2 * idx + u
                        n = 0
                        for kt in range(KT):
                            cols = slice(P * t, P * t + P)
                            for a, w in passes(xt_hi[:, kt, cols], xt_lo[:, kt, cols], w_hi["v"][:, kt], w_lo["v"][:, kt]):
                                last = pe.matmul(out[:, 256 * u:256 * u + 256], a, w, start=n == 0, stop=n == 5)
                                n += 1
                    last.then_inc(v_filled, 1)
                    return
                for two in range(2):
                    n = 0
                    for kt in range(KT):
                        cols, toks = slice(P * two, P * two + P), slice(256 * idx, 256 * idx + 256)
                        for w, a in passes(w_hi[kind][:, kt, cols], w_lo[kind][:, kt, cols], xt_hi[:, kt, toks], xt_lo[:, kt, toks]):
                            last = pe.matmul(out[:, 256 * two:256 * two + 256], w, a, start=n == 0, stop=n == 5)
                            n += 1
                last.then_inc(qk_filled, 1)

            def bank_free_alone(n, w):
                if w == 0 and n < NPAIR:
                    pe.wait_ge(v_raw_done, 4 * n + 4)
                pe.wait_ge(out_added, 8 * n + max(w - 1, 0 if n < NPAIR else -1) + OUT_ADDED_CREDIT)

            def fill_out(w, final):
                h = 1 if w < 4 else 0
                for u in range(2):
                    cols = slice(P * (2 * (w % 2) + u), P * (2 * (w % 2) + u) + P)
                    n = 0
                    for a, ww in passes(ctx_hi[:, cols], ctx_lo[:, cols], w_hi["o"][:, h], w_lo["o"][:, h]):
                        last = pe.matmul(ps_f[:, bank("o", w, None, final), D * u:D * u + D], a, ww, start=n == 0, stop=n == 2)
                        n += 1
                last.then_inc(out_filled, 1)

            def scores(n, s, which):
                h, i = divmod(s, NT)
                ci, c, k = chunks(s)[which]
                pe.wait_ge(exp_done, NCHUNK * n + ci - 2 + EXP_DONE_CREDIT)
                j = 0
                for q, kk in passes(qk_hi[:, 0, h, P * i:P * i + P], qk_lo[:, 0, h, P * i:P * i + P],
                                    qk_hi[:, 1, h, CH * c:CH * c + k], qk_lo[:, 1, h, CH * c:CH * c + k]):
                    last = pe.matmul(ps_s[:, ci % 3, 0:k], q, kk, start=j == 0, stop=j == 2)
                    j += 1
                last.then_inc(scored, 1)

            def turn(n, s, which):
                ci, c, k = chunks(s)[which]
                pe.wait_ge(exp_done, NCHUNK * n + ci + 1 + EXP_DONE_CREDIT)
                pe.wait_ge(pt_lo_done, NCHUNK * n + ci - 1 + PT_LO_DONE_CREDIT)
                for j in range(k // P):
                    last = pe.transpose(ps_t[:, ci % 2, P * j:P * j + P], probs[:, s % 2, CH * c + P * j:CH * c + P * j + P], idn[:, :])
                last.then_inc(p_turned, 1)

            def context(h, c, blocks):
                final = 4 * c + 3
                for j in blocks:
                    first = max(0, P * (j - 4 * c))
                    v = (v_hi[:, j, HD * h:HD * h + HD], v_lo[:, j, HD * h:HD * h + HD])
                    p_ = (pt_hi[c][:, j, first:], pt_lo[c][:, j, first:])
                    for m, (a, b) in enumerate(passes(*v, *p_)):
                        last = pe.matmul(ps_c[:, first:], a, b, start=j == 0 and m == 0, stop=j == final and m == 2)
                if final in blocks:
                    last.then_inc(pv_done, 1)

            def add_context(n, h, i):
                if i == 0:
                    pe.wait_ge(ctx_lo_done, 4 * n + 2 * h + CTX_LO_DONE_CREDIT)
                    pe.wait_ge(pt_lo_done, NCHUNK * n + 12 * h + PT_LO_DONE_CREDIT)
                if i == 4:
                    pe.wait_ge(ctx_lo_done, 4 * n + 2 * h + 1 + CTX_LO_DONE_CREDIT)
                    pe.wait_ge(pt_lo_done, NCHUNK * n + 12 * h + 4 + PT_LO_DONE_CREDIT)
                    pe.wait_ge(v_lo_done, 2 * n + h + 1)
                if i < 4:
                    context(1 - h, 1, (2 * i, 2 * i + 1))
                else:
                    context(h, 0, (i - 4,))

            def body(n, b, kind_of_body):
                for s in range(STEPS):
                    h, i = divmod(s, NT)
                    m, nxt = (n, s + 1) if s + 1 < STEPS else (n + 1, 0)
                    if s == 3:
                        pe.wait_ge(qk_lo_done, QK_BEFORE + 8 * n)
                    if s in (7, 11):
                        pe.wait_ge(qk_lo_done, QK_BEFORE + 8 * n + (2 if s == 7 else 4))
                    if s == STEPS - 1 and not ends(s, kind_of_body):
                        pe.wait_ge(qk_lo_done, QK_BEFORE + 8 * n + 6)
                    if not ends(s, kind_of_body):
                        scores(m, nxt, 0)
                    if s in QKV_FILLS and kind_of_body != "final":
                        kind, idx = QKV_FILLS[s]
                        if kind == "q" and idx in (0, 2) and kind_of_body == "last":
                            pe.wait_ge(xt_in[idx // 2], 32 * b + 64)
                        if idx == 0:
                            pe.wait_ge(w_lo_done, {"q": 4 * n + 4, "k": 4 * n + 5, "v": W_BEFORE + 4 * n + 1}[kind])
                        bank_free(n, kind, idx)
                        fill(n + 1, kind, idx)
                    if i % 4:
                        add_context(n, h, i)
                    turn(n, s, 0)
                    if len(chunks(nxt)) > 1:
                        scores(m, nxt, 1)
                    if s in OUT_FILLS:
                        w = OUT_FILLS[s]
                        if w % 2 == 0:
                            pe.wait_ge(ctx_lo_done, 4 * n + w // 2 + CTX_LO_DONE_CREDIT)
                        if w == 4:
                            pe.wait_ge(w_lo_done, W_BEFORE + 4 * n + (1 if kind_of_body == "final" else W_INDEX["o"] + 1))
                        if kind_of_body == "final":
                            bank_free_alone(n, w)
                        else:
                            bank_free(n, "o", w)
                        fill_out(w, kind_of_body == "final")
                    if len(chunks(s)) > 1:
                        turn(n, s, 1)
                    if i % 4 == 0:
                        add_context(n, h, i)

            pe.sem_inc(out_filled, OUT_FILLED_CREDIT)
            pe.sem_inc(p_turned, P_TURNED_CREDIT)
            order = QKV_ORDER
            for at, (kind, idx) in enumerate(order):
                if kind == "q" and idx in (0, 2):
                    pe.wait_ge(xt_in[idx // 2], 32)
                if idx == 0:
                    pe.wait_ge(w_lo_done, "qkv".index(kind) + 1)
                if at >= 2:
                    before, j = order[at - 2]
                    if before == "v":
                        pe.wait_ge(v_raw_done, j + 1)
                    else:
                        pe.wait_ge(prod_done, QK_ORDER.index((before, j)) + 1)
                fill(0, kind, idx)
            pe.wait_ge(const_in, 32)
            pe.wait_ge(qk_lo_done, 2)
            scores(0, 0, 0)
            pe.wait_ge(v_raw_done, 4)
            pe.wait_ge(zeroed, 9)
            batches(pe, body)
            n = NPAIR
            for w in range(2):
                pe.wait_ge(ctx_lo_done, 4 * n + CTX_LO_DONE_CREDIT)
                bank_free_alone(n, w)
                fill_out(w, True)
            pe.wait_ge(pt_lo_done, NCHUNK * n + PT_LO_DONE_CREDIT)
            context(1, 1, range(8))
            for w in range(2, 4):
                pe.wait_ge(ctx_lo_done, 4 * n + 1 + CTX_LO_DONE_CREDIT)
                bank_free_alone(n, w)
                fill_out(w, True)


def constants():
    freqs = 1.0 / 10000.0 ** (np.arange(0, HD, 2, dtype=np.float32) / HD)
    ang = np.outer(np.arange(S, dtype=np.float32), freqs)
    table = np.stack([np.cos(ang), np.sin(ang)]).transpose(2, 0, 1)
    table = table.reshape(HALF, 2, 4, 256).transpose(0, 2, 1, 3)
    return {
        "rope": np.ascontiguousarray(np.concatenate([table, table]), dtype=np.float32),
        "mask": np.triu(np.full((P, P), NEG, np.float32), 1),
        "ident": np.eye(P, dtype=np.float32),
    }


_INS = ['L0_attn_x', 'L0_attn_Wq', 'L0_attn_Wk', 'L0_attn_Wv', 'L0_attn_Wo', 'L0_ffn_gate_up_proj', 'L0_ffn_down_proj']


def macaron(nc, x, wq, wk, wv, wo, gate_up, down, rope, mask, ident, out):
    x1 = nc.dram_tensor("x1", [B, S, D], F32).ap()
    x2 = nc.dram_tensor("x2", [B, S, D], F32).ap()
    xnt = nc.dram_tensor("xnt", [B, 2, P, KT * S], F32).ap().rearrange("b h p (k t) -> b h p k t", k=KT)
    ffn_stage(nc, "ffn1_", x, x1, gate_up, down, ident, xnt)
    attention_stage(nc, x1, x2, xnt, wq, wk, wv, wo, rope, mask, ident)
    ffn_stage(nc, "ffn2_", x2, out, gate_up, down, ident, None)


def kernel(**inputs):
    import numpy as _np
    import concourse.bacc as _bacc
    from concourse import mybir as _mybir
    from concourse.bass_utils import run_bass_kernel_spmd as _run

    nc = _bacc.Bacc("TRN2", target_bir_lowering=False, num_devices=1)
    arrays, args = {}, []
    for name, value in [(name, inputs[name]) for name in _INS] + list(constants().items()):
        a = _np.ascontiguousarray(value)
        arrays[f"in_{name}_dram"] = a
        args.append(nc.dram_tensor(f"in_{name}_dram", a.shape, _mybir.dt.from_np(a.dtype), kind="ExternalInput").ap())
    args.append(nc.dram_tensor("out_0_dram", (B, S, D), F32, kind="ExternalOutput").ap())
    macaron(nc, *args)
    r = _run(nc, [arrays], core_ids=[0])
    return r.results[0]["out_0_dram"]
```
